# Optimizing a Trainium2 kernel written in Bass

```python
import numpy as np
import jax
import jax.numpy as jnp

def _softmax(x, axis=-1):
    return jax.nn.softmax(x, axis=axis)

def _gelu(x):
    return jax.nn.gelu(x, approximate=True)

def _silu(x):
    return jax.nn.silu(x)

def _sigmoid(x):
    return jax.nn.sigmoid(x)

def _layernorm(x, axis=-1, eps=1e-05):
    m = jnp.mean(x, axis=axis, keepdims=True)
    v = jnp.var(x, axis=axis, keepdims=True)
    return (x - m) / jnp.sqrt(v + eps)

def _scatter_add(tgt, idx, src, axis=0):
    return tgt.at[idx].add(src)

def _segment_sum(src, seg, n):
    return jax.ops.segment_sum(src, seg, n)
kernel_name = 'mk_flamingo_gated_d1_seqx_r4_4d35fd'

def setup_inputs(seed: int=0):
    np.random.seed(seed)
    _w = jnp.asarray

    def _rec_inputs():
        import jax
        import jax.numpy as jnp
        _rk = jax.random.key(seed)
        x = 7.22e-05 + 1 * jax.random.normal(jax.random.fold_in(_rk, 1), (16, 128, 512), jnp.float32)
        _lenS = 128 - jax.random.randint(jax.random.fold_in(_rk, 7), (16,), 0, max(1, 128 // 4) + 1, jnp.int32)
        _lenS2 = 128 - jax.random.randint(jax.random.fold_in(_rk, 8), (16,), 0, max(1, 128 // 4) + 1, jnp.int32)
        _ctx_2048P = jax.random.normal(jax.random.fold_in(_rk, 11), (16, 16, 512), jnp.float32)
        _ctx_2048c = jax.random.dirichlet(jax.random.fold_in(_rk, 511), 0.3 * jnp.ones((16,), jnp.float32), (16, 128))
        _ctx_2048t = jnp.einsum('bsk,bkd->bsd', _ctx_2048c, _ctx_2048P)
        _ctx_2048t = _ctx_2048t * jax.lax.rsqrt(jnp.mean(jnp.square(_ctx_2048t)) + 1e-12) * 0.953939
        ctx_2048 = 4.13588e-05 + 0.999923 * (_ctx_2048t + 0.3 * jax.random.normal(jax.random.fold_in(_rk, 611), (16, 128, 512), jnp.float32))
        _g = jax.random.normal(jax.random.fold_in(_rk, 9001), (2, 1), jnp.float32)
        _g = jnp.sign(_g) * jnp.maximum(jnp.abs(_g), 1.0) + (_g == 0) * 1.0
        g_xattn = _g[0]
        g_ffn = _g[1]
        return (x, ctx_2048, g_xattn, g_ffn)
    x, ctx_2048, g_xattn, g_ffn = _rec_inputs()

    def _L0_xattn_setup():
        import jax, jax.numpy as jnp
        import numpy as np
        N_HEAD = 8
        key = jax.random.key(seed)
        k1, k2, k3 = jax.random.split(key, 3)
        b, d, m = (4, 256, 512)
        c, n = (256, 512)
        q = jax.random.normal(k1, (b, d, m), dtype=jnp.float32)
        k = jax.random.normal(k2, (d // d * b, d, n), dtype=jnp.float32).reshape(b, d, n)
        v = jax.random.normal(k3, (b, c, n), dtype=jnp.float32)
        return {'q': q, 'k': k, 'v': v}
    _L0_xattn_all = _L0_xattn_setup()
    _L0_xattn_in = {k: v for k, v in _L0_xattn_all.items() if k in ()}
    del _L0_xattn_all

    def _L0_ffn_setup():
        import jax, jax.numpy as jnp
        import numpy as np
        B, S, H = (2, 256, 512)
        E, F = (16, 256)
        TOP_K = 4
        SH_F = 1408
        key = jax.random.key(seed)
        ks = jax.random.split(key, 9)
        sc = 0.02
        return {'hidden_states': jax.random.normal(ks[0], (B, S, H), dtype=jnp.float32), 'w_router': jax.random.normal(ks[1], (H, E), dtype=jnp.float32) * sc, 'w_gate': jax.random.normal(ks[2], (E, H, F), dtype=jnp.float32) * sc, 'w_up': jax.random.normal(ks[3], (E, H, F), dtype=jnp.float32) * sc, 'w_down': jax.random.normal(ks[4], (E, F, H), dtype=jnp.float32) * sc, 'w_sh_gate': jax.random.normal(ks[5], (H, SH_F), dtype=jnp.float32) * sc, 'w_sh_up': jax.random.normal(ks[6], (H, SH_F), dtype=jnp.float32) * sc, 'w_sh_down': jax.random.normal(ks[7], (SH_F, H), dtype=jnp.float32) * sc, 'w_sh_expert_gate': jax.random.normal(ks[8], (H, 1), dtype=jnp.float32) * sc}
    _L0_ffn_all = _L0_ffn_setup()
    _L0_ffn_in = {k: v for k, v in _L0_ffn_all.items() if k in ('w_router', 'w_gate', 'w_up', 'w_down', 'w_sh_gate', 'w_sh_up', 'w_sh_down', 'w_sh_expert_gate')}
    del _L0_ffn_all
    return {'x': x, 'ctx_2048': ctx_2048, 'g_xattn': g_xattn, 'g_ffn': g_ffn, 'L0_ffn_w_router': _L0_ffn_in['w_router'], 'L0_ffn_w_gate': _L0_ffn_in['w_gate'], 'L0_ffn_w_up': _L0_ffn_in['w_up'], 'L0_ffn_w_down': _L0_ffn_in['w_down'], 'L0_ffn_w_sh_gate': _L0_ffn_in['w_sh_gate'], 'L0_ffn_w_sh_up': _L0_ffn_in['w_sh_up'], 'L0_ffn_w_sh_down': _L0_ffn_in['w_sh_down'], 'L0_ffn_w_sh_expert_gate': _L0_ffn_in['w_sh_expert_gate']}

def reference(x, ctx_2048, g_xattn, g_ffn, L0_ffn_w_router, L0_ffn_w_gate, L0_ffn_w_up, L0_ffn_w_down, L0_ffn_w_sh_gate, L0_ffn_w_sh_up, L0_ffn_w_sh_down, L0_ffn_w_sh_expert_gate):
    import jax
    import jax.numpy as jnp

    def _L0_xattn_ref(q, k, v):
        import jax, jax.numpy as jnp
        import numpy as np
        N_HEAD = 8
        b, d, m = q.shape
        c = v.shape[1]
        h = N_HEAD
        qh = q.reshape(b * h, d // h, m)
        kh = k.reshape(b * h, d // h, -1)
        vh = v.reshape(b * h, c // h, -1)
        scale = 1.0 / jnp.sqrt(jnp.asarray(d // h, dtype=q.dtype))
        qk = jnp.einsum('bdm,bdn->bmn', qh, kh) * scale
        sm = jax.nn.softmax(qk, axis=-1)
        ret = jnp.einsum('bmn,bcn->bcm', sm, vh)
        return ret.reshape(b, c, m)

    def _L0_ffn_ref(hidden_states, w_router, w_gate, w_up, w_down, w_sh_gate, w_sh_up, w_sh_down, w_sh_expert_gate):
        import jax, jax.numpy as jnp
        import numpy as np
        B, S, H = (2, 256, 512)
        E, F = (16, 256)
        TOP_K = 4
        SH_F = 1408
        b, s, h = hidden_states.shape
        x = hidden_states.reshape(-1, h)
        router_logits = x @ w_router
        probs = jax.nn.softmax(router_logits, axis=-1)
        topk_w, topk_ids = jax.lax.top_k(probs, TOP_K)
        topk_w = topk_w / jnp.sum(topk_w, axis=-1, keepdims=True)
        combine = jnp.sum(jax.nn.one_hot(topk_ids, E, dtype=x.dtype) * topk_w[..., None], axis=1)
        g = jnp.einsum('th,ehf->tef', x, w_gate)
        u = jnp.einsum('th,ehf->tef', x, w_up)
        act = jax.nn.silu(g) * u
        act = act * combine[:, :, None]
        moe_out = jnp.einsum('tef,efh->th', act, w_down)
        sg = jax.nn.silu(x @ w_sh_gate) * (x @ w_sh_up)
        shared = sg @ w_sh_down
        gate = jax.nn.sigmoid(x @ w_sh_expert_gate)
        out = moe_out + gate * shared
        return out.reshape(b, s, h)
    x = x + jnp.tanh(g_xattn[0]) * _L0_xattn_ref(_layernorm(x, axis=-1), ctx_2048, ctx_2048)
    x = x + jnp.tanh(g_ffn[0]) * _L0_ffn_ref(_layernorm(x, axis=-1), L0_ffn_w_router, L0_ffn_w_gate, L0_ffn_w_up, L0_ffn_w_down, L0_ffn_w_sh_gate, L0_ffn_w_sh_up, L0_ffn_w_sh_down, L0_ffn_w_sh_expert_gate)
    return x

_drawn_inputs = setup_inputs


def setup_inputs(seed=0):
    import zlib

    import numpy as np

    out = dict(_drawn_inputs(seed))
    spreads = {}
    factors = {'L0_ffn_w_router': 4.691,
     'L0_ffn_w_gate': 4.178,
     'L0_ffn_w_up': 4.091,
     'L0_ffn_w_down': 4.087,
     'L0_ffn_w_sh_expert_gate': 8.0}
    for name, (base, spread) in spreads.items():
        noise = np.random.default_rng([zlib.crc32(name.encode()), seed]).standard_normal(out[name].shape)
        drawn = base * np.exp(spread * noise) if base else spread * noise
        out[name] = jnp.asarray(drawn.astype(out[name].dtype))
    for name, factor in factors.items():
        out[name] = (out[name] * factor).astype(out[name].dtype)
    return out
```

```python
from contextlib import ExitStack

import concourse.bass as bass
from concourse import mybir

F32 = mybir.dt.float32
F32R = mybir.dt.float32r
U32 = mybir.dt.uint32
ALU = mybir.AluOpType
ACT = mybir.ActivationFunctionType
AX_X = mybir.AxisListType.X
P = 128


class Group:

    def __init__(self, q, r):
        self.q, self.r, self.g = q, r, 4 * r + q
        self.first = isinstance(r, int) and r == 0

    def known(self):
        return isinstance(self.r, int)

    def at_least(self, n):
        return not self.known() or self.g >= n

    def before(self, n):
        return not self.known() or self.g < n


def gated_block(nc, x, ctx_in, g_xattn, g_ffn, w_router, w_gate, w_up, w_down, ws_gate, ws_up, ws_down, w_eg, out):
    B, TOK, D = x.shape
    NE, _, FE = w_gate.shape
    FS = ws_gate.shape[1]
    HEADS = 8
    HD = TOK // HEADS
    HG = 4
    GR = HG * HD
    NG = B * HEADS // HG
    KC = D // P
    SCALE = float(HD) ** -0.5
    EPS = 1e-5
    ROWS = 3 * HD
    PAD = 96
    TOP = 4
    NCOL = NE + 1
    assert TOK == P and D == 512 and KC == 4 and HG * 32 == P and NG == 32 and FE == 256 and TOP == KC

    with ExitStack() as whole:
        def sem(name):
            return whole.enter_context(nc.semaphore(name))

        def held(stack, name, shape, dt=F32):
            return stack.enter_context(nc.sbuf_tensor(name, shape, dt))

        y_all = held(whole, "y_all", [P, B * D])
        yn_t = held(whole, "yn_t", [P, 2, KC, B * TOK], F32R)
        logits = held(whole, "logits", [P, B, NCOL])
        tanh_g = held(whole, "tanh_g", [P, 2])

        attn = ExitStack()
        whole.enter_context(attn)
        sb = lambda name, shape, dt=F32: held(attn, name, shape, dt)
        ps = lambda name, shape, dt=F32: attn.enter_context(nc.psum_tensor(name, shape, dt))

        q_stack = [sb(f"q_stack{i}", [P, HG, D], F32R) for i in range(4)]
        k_stack = [sb(f"k_stack{i}", [P, HG, D], F32R) for i in range(4)]
        probs = sb("probs", [P, 2, HG, D])
        v_rows = [sb(f"v_rows{i}", [GR, D]) for i in range(2)]
        v_t = [sb(f"v_t{i}", [P, KC, HG, 32]) for i in range(2)]
        maxima = [sb(f"maxima{i}", [P, 4 * HG]) for i in range(2)]
        max_hi = sb("max_hi", [4 * HG, P], F32R)
        max_lo = sb("max_lo", [4 * HG, P], F32R)
        o_sb = sb("o_sb", [P, D])
        recip = sb("recip", [P, KC, HG, 1])
        attn_t = sb("attn_t", [P, KC, TOK])
        x_res = [sb(f"x_res{i}", [P, D]) for i in range(2)]
        yn = sb("yn", [P, D])
        yn32 = sb("yn32", [P, KC, TOK])
        w_r = sb("w_r", [P, KC, NCOL])
        ident = sb("ident", [P, P])
        neg_one = sb("neg_one", [2, HG * D])
        expo = sb("expo", [P, 1])
        g_raw = sb("g_raw", [P, 2])
        bn = sb("bn", [P, 2, 6])
        mean_var = [sb(f"mean_var{i}", [P, 2]) for i in range(2)]
        var_eps = [sb(f"var_eps{i}", [P, 1]) for i in range(2)]
        rstd = [sb(f"rstd{i}", [P, 1]) for i in range(2)]
        bn2 = sb("bn2", [P, 6])
        mean_var2 = sb("mean_var2", [P, 2])
        var_eps2 = sb("var_eps2", [P, 1])
        rstd2 = sb("rstd2", [P, 1])

        part = lambda tile, n: tile[:, n * D:(n + 1) * D]
        x_in, k_in, xn = ([part(y_all, 2 * i + j) for j in range(2)] for i in range(3))
        yn_flat = yn_t[:, :, :, :].rearrange("p a k t -> p (a k t)")
        q_hi, q_lo, k_hi, k_lo = ([part(yn_flat, 2 * i + j) for j in range(2)] for i in range(4))

        sa_ps = ps("sa_ps", [P, 2, 2, D])
        sb_ps = ps("sb_ps", [P, 2, D])
        o_ps = ps("o_ps", [P, D])
        m_ps = ps("m_ps", [P, D])

        halves = {n: nc.dram_tensor(f"{n}_dram", (B, HEADS, HD, D), F32, kind="Internal").ap()
                  for n in ("q_hi", "q_lo", "k_hi", "k_lo")}

        s_const, s_setup, s_small, s_tanh = sem("s_const"), sem("s_setup"), sem("s_small"), sem("s_tanh")
        x_loaded = [sem(f"x_loaded{i}") for i in range(2)]
        k_loaded = [sem(f"k_loaded{i}") for i in range(2)]
        halves_stored = [sem(f"halves_stored{i}") for i in range(2)]
        bn_done, mv_done, ve_done, rstd_done, xn_done = (sem(n) for n in ("bn_done", "mv_done", "ve_done", "rstd_done", "xn_done"))
        q_hi_done, q_lo_done, k_hi_done, k_lo_done = (sem(n) for n in ("q_hi_done", "q_lo_done", "k_hi_done", "k_lo_done"))
        stack_loaded = [sem(f"stack_loaded{i}") for i in range(4)]
        max_rows = [sem(f"max_rows{i}") for i in range(4)]
        v_loaded = [sem(f"v_loaded{i}") for i in range(2)]
        res_loaded = [sem(f"res_loaded{i}") for i in range(2)]
        y_kept = [sem(f"y_kept{i}") for i in range(2)]
        sa_done = sem("sa_done")
        max_done = sem("max_done")
        vm_done = sem("vm_done")
        mhi_done, mlo_done, vt_done = sem("mhi_done"), sem("mlo_done"), sem("vt_done")
        sb_done = sem("sb_done")
        exp_done = sem("exp_done")
        pv_done = sem("pv_done")
        o_done = sem("o_done")
        ot_done, rc_done, norm_done = sem("ot_done"), sem("rc_done"), sem("norm_done")
        back_done, y_done = sem("back_done"), sem("y_done")
        bn2_done, mv2_done, ve2_done, rstd2_done, yn_done = (sem(n) for n in ("bn2_done", "mv2_done", "ve2_done", "rstd2_done", "yn_done"))
        ynt_done, yn32_done, ynhi_done, ynlo_done = (sem(n) for n in ("ynt_done", "yn32_done", "ynhi_done", "ynlo_done"))
        router_done, logits_done = sem("router_done"), sem("logits_done")

        def batch_back(s):
            return 2 * s.r - 1 if s.q == 0 else 2 * s.r

        def batch_late(s):
            return 2 * s.r - 1 if s.q == 1 else 2 * s.r

        def has_back(s):
            return s.q % 2 == 0 and s.at_least(2)

        def has_late(s):
            return s.q % 2 == 1 and s.at_least(3)

        def slots(eng, slot):
            for g in range(3):
                slot(Group(g, 0))
            with eng.Fori(0, 6) as i:
                for q in (3, 4, 5, 6):
                    slot(Group(q % 4, i + q // 4))
            for g in range(27, NG):
                slot(Group(g % 4, g // 4))

        block = attn.enter_context(nc.Block())

        @block.sync
        def _(sp):
            def load_rows(b, j, waits):
                if waits:
                    sp.wait_ge(xn_done, b - 1)
                sp.dma_start(x_in[j], x[b]).then_inc(x_loaded[j], 16)
                if waits:
                    sp.wait_ge(k_lo_done, b - 1)
                sp.dma_start(k_in[j], ctx_in[b]).then_inc(k_loaded[j], 16)

            def store_halves(b, j):
                for name, tile, done in (("k_hi", k_hi, k_hi_done), ("k_lo", k_lo, k_lo_done),
                                         ("q_hi", q_hi, q_hi_done), ("q_lo", q_lo, q_lo_done)):
                    sp.wait_ge(done, b + 1)
                    sp.dma_start(halves[name][b].rearrange("h e d -> (h e) d"), tile[j].bitcast(F32)).then_inc(halves_stored[j], 16)

            for j in range(2):
                load_rows(j, j, False)
            with sp.Fori(0, B // 2 - 1) as t:
                for j in range(2):
                    load_rows(2 * t + 2 + j, j, True)
                for j in range(2):
                    store_halves(2 * t + j, j)
            for j in range(2):
                store_halves(B - 2 + j, j)

            def load_values(g_of, j, b, half):
                sp.dma_start(v_rows[j][:, :], ctx_in[b][half * GR:(half + 1) * GR, :]).then_inc(v_loaded[j], 16)

            def load_stack(i, b, half, stored):
                sp.wait_ge(halves_stored[half_of_pair(i)], stored)
                for stack, names in ((q_stack, ("q_hi", "q_hi", "q_lo")), (k_stack, ("k_hi", "k_lo", "k_hi"))):
                    for n, name in enumerate(names):
                        src = halves[name][b][half * HG:(half + 1) * HG].rearrange("h e d -> e h d")
                        sp.dma_start(stack[i][n * HD:(n + 1) * HD, :, :].bitcast(F32), src).then_inc(stack_loaded[i], 16)

            def half_of_pair(i):
                return i // 2

            def store_max_rows(i, g):
                sp.wait_ge(mhi_done, g + 1)
                sp.dma_start(q_stack[i][PAD:PAD + 1, :, :].bitcast(F32), max_hi[:, :].bitcast(F32)).then_inc(max_rows[i], 16)
                sp.wait_ge(mlo_done, g + 1)
                sp.dma_start(q_stack[i][PAD + 1:PAD + 2, :, :].bitcast(F32), max_lo[:, :].bitcast(F32)).then_inc(max_rows[i], 16)

            load_values(0, 0, 0, 0)
            load_values(1, 1, 0, 1)
            for g in range(4):
                load_stack(g, g // 2, g % 2, 64)
            store_max_rows(0, 0)

            def keep_y(b, j):
                sp.wait_ge(yn_done, b + 1)
                sp.dma_start(y_all[:, bass.ds(b * D, D)], x_res[j][:, :]).then_inc(y_kept[j], 16)

            def slot(s):
                if s.before(NG - 2):
                    sp.wait_ge(vm_done, s.g + 1)
                    load_values(s.g + 2, s.q % 2, 2 * s.r + s.q // 2 + 1, s.q % 2)
                if s.q % 2 == 0:
                    b, j = 2 * s.r + s.q // 2, s.q // 2
                    if s.at_least(4):
                        keep_y(b - 2, j)
                        sp.wait_ge(y_kept[j], 16 * s.r)
                    sp.dma_start(x_res[j][:, :], x[b]).then_inc(res_loaded[j], 16)
                if s.before(NG - 1):
                    store_max_rows((s.q + 1) % 4, s.g + 1)
                if s.before(NG - 4):
                    sp.wait_ge(sb_done, 16 * s.g + 16)
                    load_stack(s.q, 2 * s.r + 2 + s.q // 2, s.q % 2, 64 * s.r + 128)

            slots(sp, slot)
            for j in range(2):
                keep_y(B - 2 + j, j)
            for j in range(2):
                sp.wait_ge(y_kept[j], 16 * (B // 2))

        @block.gpsimd
        def _(pool):
            pool.memset(ident[:, :], 0.0).then_inc(s_const, 1)
            pool.memset(expo[:, :], -0.5).then_inc(s_const, 1)
            pool.memset(probs[:, 0, :, :], 0.0).then_inc(s_const, 1)
            pool.memset(neg_one[:, :], -1.0).then_inc(s_const, 1)
            pool.wait_ge(s_const, 4)
            pool.affine_select(out=ident[:, :], in_=ident[:, :], compare_op=ALU.not_equal, fill=1.0,
                               base=0, pattern=[[-1, P]], channel_multiplier=1).then_inc(s_const, 1)
            for j in range(2):
                pool.memset(v_t[j][:, :, :, :], 0.0).then_inc(s_const, 1)
            pool.wait_ge(s_const, 7)
            for j in range(2):
                pool.memset(v_t[j][:, :, :, HD:HD + 1], 1.0).then_inc(s_const, 1)

            def prepare(t):
                for j in range(2):
                    pool.wait_ge(ve_done, 2 * t + j + 1)
                    pool.tensor_tensor(rstd[j][:, :], var_eps[j][:, :], expo[:, :], ALU.pow).then_inc(rstd_done, 1)
                for j in range(2):
                    pool.wait_ge(k_hi_done, 2 * t + j + 1)
                    pool.tensor_tensor(k_lo[j], k_in[j], k_hi[j].bitcast(F32), ALU.subtract).then_inc(k_lo_done, 1)

            with pool.Fori(0, B // 2) as t:
                prepare(t)
            for j in range(2):
                pool.wait_ge(halves_stored[j], 64 * (B // 2))

            def reciprocal_deviation(b):
                pool.wait_ge(ve2_done, b + 1)
                pool.tensor_tensor(rstd2[:, :], var_eps2[:, :], expo[:, :], ALU.pow).then_inc(rstd2_done, 1)

            def split_yn(b):
                at = bass.ds(b * TOK, TOK)
                pool.wait_ge(ynhi_done, b + 1)
                pool.tensor_tensor(yn_t[:, 1, :, at], yn32[:, :, :], yn_t[:, 0, :, at].bitcast(F32),
                                   ALU.subtract).then_inc(ynlo_done, 1)

            def slot(s):
                if has_late(s):
                    reciprocal_deviation(batch_late(s))
                    split_yn(batch_late(s))

            slots(pool, slot)
            reciprocal_deviation(B - 1)
            split_yn(B - 1)

        @block.scalar
        def _(act):
            act.wait_ge(s_const, 4)
            for i in range(4):
                zeros = probs[0:PAD - ROWS, 0, :, :]
                act.dma_start(q_stack[i][ROWS:PAD, :, :].bitcast(F32), zeros).then_inc(s_setup, 16)
                act.dma_start(k_stack[i][ROWS:PAD, :, :].bitcast(F32), zeros).then_inc(s_setup, 16)
                act.dma_start(k_stack[i][PAD:PAD + 2, :, :].bitcast(F32),
                              neg_one[:, :].rearrange("p (h d) -> p h d", h=HG)).then_inc(s_setup, 16)
            act.dma_start(w_r[:, :, 0:NE], w_router.rearrange("(k p) e -> p k e", p=P)).then_inc(s_small, 16)
            act.dma_start(w_r[:, :, NE:NCOL], w_eg.rearrange("(k p) e -> p k e", p=P),
                          allow_slow_non_contiguous=True).then_inc(s_small, 16)
            act.dma_start(g_raw[:, 0:1], g_xattn.partition_broadcast(P)).then_inc(s_small, 16)
            act.dma_start(g_raw[:, 1:2], g_ffn.partition_broadcast(P)).then_inc(s_small, 16)
            act.wait_ge(s_small, 64)
            act.activation(tanh_g[:, :], g_raw[:, :], ACT.Tanh).then_inc(s_tanh, 1)

            def prepare(t):
                for j in range(2):
                    act.wait_ge(k_loaded[j], 16 * t + 16)
                    if not isinstance(t, int):
                        act.wait_ge(halves_stored[j], 64 * t)
                    act.activation(k_hi[j], k_in[j], ACT.Copy).then_inc(k_hi_done, 1)
                for j in range(2):
                    act.wait_ge(xn_done, 2 * t + j + 1)
                    act.activation(q_hi[j], xn[j], ACT.Copy).then_inc(q_hi_done, 1)

            prepare(0)
            with act.Fori(1, B // 2) as t:
                prepare(t)
            act.wait_ge(s_setup, 16 * 12)

            def copy_out(g):
                act.wait_ge(pv_done, 4 * g + 4)
                act.wait_ge(ot_done, g)
                act.activation(o_sb[:, :], o_ps[:, :], ACT.Copy).then_inc(o_done, 1)

            def copy_yn(b):
                act.wait_ge(ynt_done, b + 1)
                act.wait_ge(router_done, b)
                act.wait_ge(ynlo_done, b)
                act.activation(yn32[:, :, :].rearrange("p k t -> p (k t)"), m_ps[:, :], ACT.Copy).then_inc(yn32_done, 1)

            def slot(s):
                for c in range(KC):
                    if c == 2 and has_late(s):
                        copy_yn(batch_late(s))
                    for j in range(HG):
                        n = 16 * s.g + HG * c + j
                        act.wait_ge(sb_done, n + 1)
                        if j == 0 and (c >= 2 or s.at_least(1)):
                            act.wait_ge(pv_done, 4 * s.g + c - 1)
                        act.activation(probs[:, c % 2, j, :], sb_ps[:, j % 2, :], ACT.Exp, scale=SCALE).then_inc(exp_done, 1)
                    if c == 0 and s.at_least(1):
                        copy_out(s.g - 1)

            slots(act, slot)
            copy_out(NG - 1)
            copy_yn(B - 1)

        @block.vector
        def _(dve):
            def prepare(t):
                dve.wait_ge(x_loaded[0], 16 * t + 16)
                dve.bn_stats(bn[:, 0, :], x_in[0]).then_inc(bn_done, 1)
                dve.wait_ge(x_loaded[1], 16 * t + 16)
                dve.wait_ge(bn_done, 2 * t + 1)
                dve.bn_stats(bn[:, 1, :], x_in[1]).then_inc(bn_done, 1)
                dve.bn_aggr(mean_var[0][:, :], bn[:, 0, :]).then_inc(mv_done, 1)
                dve.wait_ge(mv_done, 2 * t + 1)
                dve.wait_ge(bn_done, 2 * t + 2)
                dve.tensor_scalar(var_eps[0][:, :], mean_var[0][:, 1:2], EPS, None, ALU.add).then_inc(ve_done, 1)
                dve.bn_aggr(mean_var[1][:, :], bn[:, 1, :]).then_inc(mv_done, 1)
                dve.wait_ge(mv_done, 2 * t + 2)
                dve.tensor_scalar(var_eps[1][:, :], mean_var[1][:, 1:2], EPS, None, ALU.add).then_inc(ve_done, 1)
                for j in range(2):
                    b = 2 * t + j
                    dve.wait_ge(rstd_done, b + 1)
                    if not isinstance(t, int):
                        dve.wait_ge(q_hi_done, b - 1)
                    dve.tensor_scalar(xn[j], x_in[j], mean_var[j][:, 0:1], rstd[j][:, 0:1],
                                      ALU.subtract, ALU.mult).then_inc(xn_done, 1)
                for j in range(2):
                    dve.wait_ge(q_hi_done, 2 * t + j + 1)
                    dve.tensor_tensor(q_lo[j], xn[j], q_hi[j].bitcast(F32), ALU.subtract).then_inc(q_lo_done, 1)

            prepare(0)
            with dve.Fori(1, B // 2) as t:
                prepare(t)
            dve.wait_ge(s_const, 9)
            dve.wait_ge(s_tanh, 1)
            dve.wait_ge(k_lo_done, B)

            def unit(q, g, u):
                n = 8 * g + u
                dve.wait_ge(sa_done, n + 1)
                if u == 0 and not (isinstance(g, int) and g < 2):
                    dve.wait_ge(vm_done, g - 1)
                dve.tensor_reduce(maxima[q % 2][:, 2 * u:2 * u + 2], sa_ps[:, u % 2, :, :], AX_X, ALU.max).then_inc(max_done, 1)

            def values_and_maxima(q, g):
                dve.wait_ge(vm_done, g + 1)
                if not (isinstance(g, int) and g == 0):
                    rows = max_rows[(q - 1) % 4]
                    dve.wait_ge(rows, 32 * ((g - 1) // 4 if isinstance(g, int) else rows_of(q, g)) + 32)
                dve.tensor_copy(max_hi[:, :], m_ps[0:4 * HG, 256:384]).then_inc(mhi_done, 1)
                dve.wait_ge(mhi_done, g + 1)
                dve.tensor_tensor(max_lo[:, :], m_ps[0:4 * HG, 256:384], max_hi[:, :].bitcast(F32), ALU.subtract).then_inc(mlo_done, 1)
                if not (isinstance(g, int) and g < 2):
                    dve.wait_ge(pv_done, 4 * g - 4)
                dve.tensor_copy(v_t[q % 2][:, :, :, 0:HD],
                                m_ps[:, 0:KC * GR].rearrange("p (k h e) -> p k h e", k=KC, h=HG)).then_inc(vt_done, 1)

            r_of = {}

            def rows_of(q, g):
                return r_of["now"]

            def normalise(q, g):
                view = m_ps[:, :].rearrange("p (k h e) -> p k h e", k=KC, h=HG)
                dve.wait_ge(ot_done, g + 1)
                dve.reciprocal(recip[:, :, :, :], view[:, :, :, HD:HD + 1]).then_inc(rc_done, 1)
                if q % 2 == 0 and not (isinstance(g, int) and g == 0):
                    dve.wait_ge(back_done, batch_of(q, g))
                dve.wait_ge(rc_done, g + 1)
                dst = attn_t[:, :, (q % 2) * GR:(q % 2 + 1) * GR].rearrange("p k (h e) -> p k h e", h=HG)
                dve.tensor_tensor(dst, view[:, :, :, 0:HD], recip[:, :, :, :].to_broadcast([P, KC, HG, HD]),
                                  ALU.mult).then_inc(norm_done, 1)

            def batch_of(q, g):
                return g // 2 if isinstance(g, int) else r_of["batch"]

            def residual(b, j):
                dve.wait_ge(back_done, b + 1)
                dve.wait_ge(res_loaded[j], 16 * r_of["pair"] + 16)
                dve.scalar_tensor_tensor(out=x_res[j][:, :], in0=m_ps[:, :], scalar=tanh_g[:, 0:1], in1=x_res[j][:, :],
                                         op0=ALU.mult, op1=ALU.add).then_inc(y_done, 1)
                dve.wait_ge(y_done, b + 1)
                dve.bn_stats(bn2[:, :], x_res[j][:, :]).then_inc(bn2_done, 1)

            def variance(b):
                dve.bn_aggr(mean_var2[:, :], bn2[:, :]).then_inc(mv2_done, 1)
                dve.wait_ge(mv2_done, b + 1)
                dve.tensor_scalar(var_eps2[:, :], mean_var2[:, 1:2], EPS, None, ALU.add).then_inc(ve2_done, 1)

            def normed(b, j):
                dve.wait_ge(rstd2_done, b + 1)
                dve.wait_ge(ynt_done, b)
                dve.tensor_scalar(yn[:, :], x_res[j][:, :], mean_var2[:, 0:1], rstd2[:, 0:1],
                                  ALU.subtract, ALU.mult).then_inc(yn_done, 1)

            def upper_half(b):
                dve.wait_ge(yn32_done, b + 1)
                dve.tensor_scalar(yn_t[:, 0, :, bass.ds(b * TOK, TOK)], yn32[:, :, :], 1.0, None, ALU.mult).then_inc(ynhi_done, 1)

            def keep_logits(b):
                dve.wait_ge(router_done, b + 1)
                dve.tensor_copy(logits[:, b, :] if isinstance(b, int) else logits[:, bass.ds(b, 1), :].rearrange("p a n -> p (a n)"),
                                m_ps[:, 0:NCOL]).then_inc(logits_done, 1)

            def slot(s):
                q, g = s.q, s.g
                q1, q2 = (q + 1) % 4, (q + 2) % 4
                if has_late(s):
                    r_of["pair"] = s.r - 1 if q == 1 else s.r
                    residual(batch_late(s), 1 if q == 1 else 0)
                    dve.wait_ge(bn2_done, batch_late(s) + 1)
                if s.before(NG - 1):
                    unit(q1, g + 1, 4)
                if has_late(s):
                    variance(batch_late(s))
                if s.before(NG - 1):
                    unit(q1, g + 1, 5)
                if has_late(s):
                    normed(batch_late(s), 1 if q == 1 else 0)
                if s.before(NG - 1):
                    unit(q1, g + 1, 6)
                if s.at_least(1):
                    r_of["batch"] = 2 * s.r + q // 2
                    normalise((q - 1) % 4, g - 1)
                if s.before(NG - 1):
                    unit(q1, g + 1, 7)
                if s.before(NG - 2):
                    unit(q2, g + 2, 0)
                if s.before(NG - 1):
                    r_of["now"] = s.r
                    values_and_maxima(q1, g + 1)
                if s.before(NG - 2):
                    unit(q2, g + 2, 1)
                    unit(q2, g + 2, 2)
                if has_late(s):
                    upper_half(batch_late(s))
                    keep_logits(batch_late(s))
                if s.before(NG - 2):
                    unit(q2, g + 2, 3)

            for u in range(8):
                unit(0, 0, u)
            unit(1, 1, 0)
            unit(1, 1, 1)
            values_and_maxima(0, 0)
            unit(1, 1, 2)
            unit(1, 1, 3)
            slots(dve, slot)
            normalise(3, NG - 1)
            r_of["pair"] = B // 2 - 1
            residual(B - 1, 1)
            dve.wait_ge(bn2_done, B)
            variance(B - 1)
            normed(B - 1, 1)
            upper_half(B - 1)
            keep_logits(B - 1)

        @block.tensor
        def _(pe):
            pe.wait_ge(s_small, 64)
            pe.wait_ge(s_const, 9)
            pe.wait_ge(s_setup, 16 * 12)

            def scores(i, g, r, u, half):
                n = 8 * g + u
                if u == 0 and half == 0:
                    pe.wait_ge(stack_loaded[i], 96 * r + 96)
                if half == 0 and not (isinstance(n, int) and n < 2):
                    pe.wait_ge(max_done, n - 1)
                at = (2 * (u % 2) + half) * P
                mm = pe.matmul(sa_ps[:, u % 2, half, :], q_stack[i][0:PAD, u // 2, at:at + P],
                               k_stack[i][0:PAD, u // 2, :], start=True, stop=True)
                if half == 1:
                    mm.then_inc(sa_done, 1)

            def scores_t(s, c, j):
                n = 16 * s.g + HG * c + j
                if c == 0 and j == 0:
                    pe.wait_ge(max_rows[s.q], 32 * s.r + 32)
                if not (isinstance(n, int) and n < 2):
                    pe.wait_ge(exp_done, n - 1)
                pe.matmul(sb_ps[:, j % 2, :], k_stack[s.q][0:PAD + 2, j, c * P:(c + 1) * P],
                          q_stack[s.q][0:PAD + 2, j, :], start=True, stop=True).then_inc(sb_done, 1)

            def by_values(q, g, c):
                if c == 0:
                    pe.wait_ge(vt_done, g + 1)
                    if not (isinstance(g, int) and g == 0):
                        pe.wait_ge(o_done, g)
                pe.wait_ge(exp_done, 16 * g + 4 * c + 4)
                for j in range(HG):
                    mm = pe.matmul(o_ps[32 * j:32 * j + 32, :], v_t[q % 2][:, c, j, :], probs[:, c % 2, j, :],
                                   start=(c == 0), stop=(c == KC - 1))
                mm.then_inc(pv_done, 1)

            def values_and_maxima(q, g):
                pe.wait_ge(v_loaded[q % 2], 16 * half_of(q, g) + 16)
                pe.wait_ge(max_done, 8 * g + 8)
                pe.transpose(m_ps[0:4 * HG, 256:384], maxima[q % 2][:, :], ident[:, :])
                for c in range(KC):
                    mm = pe.transpose(m_ps[:, c * GR:(c + 1) * GR], v_rows[q % 2][:, c * P:(c + 1) * P], ident[0:GR, 0:GR])
                mm.then_inc(vm_done, 1)

            loop = {}

            def half_of(q, g):
                return g // 2 if isinstance(g, int) else loop["pair"]

            def outputs_t(g):
                pe.wait_ge(o_done, g + 1)
                for c in range(KC):
                    mm = pe.transpose(m_ps[:, c * P:(c + 1) * P], o_sb[:, c * P:(c + 1) * P], ident[:, :])
                mm.then_inc(ot_done, 1)

            def back(b):
                pe.wait_ge(norm_done, 2 * b + 2)
                for c in range(KC):
                    mm = pe.transpose(m_ps[:, c * P:(c + 1) * P], attn_t[:, c, :], ident[:, :])
                mm.then_inc(back_done, 1)

            def normed_t(b):
                pe.wait_ge(yn_done, b + 1)
                for c in range(KC):
                    mm = pe.transpose(m_ps[:, c * P:(c + 1) * P], yn[:, c * P:(c + 1) * P], ident[:, :])
                mm.then_inc(ynt_done, 1)

            def router(b):
                pe.wait_ge(yn32_done, b + 1)
                for c in range(KC):
                    mm = pe.matmul(m_ps[:, 0:NCOL], yn32[:, c, :], w_r[:, c, :], start=(c == 0), stop=(c == KC - 1))
                mm.then_inc(router_done, 1)

            def slot(s):
                q, g, r = s.q, s.g, s.r
                q1, q2 = (q + 1) % 4, (q + 2) % 4
                for c in range(KC):
                    for j in range(HG):
                        scores_t(s, c, j)
                        u = 2 * c + j // 2 + (4 if c < 2 else -4)
                        if c < 2 and s.before(NG - 1):
                            scores(q1, g + 1, r + (q + 1) // 4, u, j % 2)
                        if c >= 2 and s.before(NG - 2):
                            scores(q2, g + 2, r + (q + 2) // 4, u, j % 2)
                        if c == 1 and j == 1 and s.at_least(1):
                            if q % 2 == 0 and s.at_least(4):
                                pe.wait_ge(logits_done, 2 * r - 1 + q // 2)
                            elif q % 2 == 1 and s.at_least(3):
                                pe.wait_ge(y_done, 2 * r + q // 2)
                            else:
                                pe.wait_ge(vt_done, g + 1)
                            outputs_t(g - 1)
                        if c == 2 and j == 1 and s.before(NG - 1):
                            if has_late(s):
                                pe.wait_ge(yn32_done, batch_late(s) + 1)
                            elif s.at_least(1):
                                pe.wait_ge(norm_done, g)
                            else:
                                pe.wait_ge(vt_done, 1)
                            loop["pair"] = pair_of(s)
                            values_and_maxima(q1, g + 1)
                        if c == 3 and j == 1 and has_back(s):
                            pe.wait_ge(vt_done, g + 2)
                            back(batch_back(s))
                    if c > 0:
                        by_values(q, g, c - 1)
                    elif s.at_least(1):
                        by_values((q - 1) % 4, g - 1, KC - 1)
                    if c == 1 and has_late(s):
                        pe.wait_ge(norm_done, g)
                        normed_t(batch_late(s))
                    if c == 2 and has_late(s):
                        if s.before(NG - 1):
                            pe.wait_ge(vt_done, g + 2)
                        router(batch_late(s))

            def pair_of(s):
                return 2 * s.r + (s.q + 1) // 2

            for u in range(8):
                for half in range(2):
                    scores(0, 0, 0, u, half)
            for u in range(2):
                for half in range(2):
                    scores(1, 1, 0, u, half)
            values_and_maxima(0, 0)
            for u in range(2, 4):
                for half in range(2):
                    scores(1, 1, 0, u, half)
            slots(pe, slot)
            by_values(3, NG - 1, KC - 1)
            pe.wait_ge(logits_done, B - 1)
            outputs_t(NG - 1)
            pe.wait_ge(norm_done, NG)
            back(B - 1)
            pe.wait_ge(y_done, B)
            normed_t(B - 1)
            router(B - 1)

        attn.close()
        experts(nc, whole, sem, y_all, yn_t, logits, tanh_g, w_gate, w_up, w_down, ws_gate, ws_up, ws_down, out)


def experts(nc, whole, sem, y_all, yn_t, logits, tanh_g, w_gate, w_up, w_down, ws_gate, ws_up, ws_down, out):
    B, TOK, D = out.shape
    NE, _, FE = w_gate.shape
    FS = ws_gate.shape[1]
    KC = D // P
    SPAN = 512
    NT = B * TOK // SPAN
    TT = SPAN // TOK
    TOP = 4
    NCOL = NE + 1
    HALF = FS % FE
    NSH = FS // FE
    NCH = 1 + NSH + NE
    assert HALF == P and NSH == 5 and FE == 2 * P and NT == 4 and TT == 4

    stack = whole.enter_context(ExitStack())
    sb = lambda name, shape, dt=F32: stack.enter_context(nc.sbuf_tensor(name, shape, dt))
    ps = lambda name, shape, dt=F32: stack.enter_context(nc.psum_tensor(name, shape, dt))

    PIECE = KC * FE
    w_raw = [sb(f"w_raw{i}", [P, 3, PIECE]) for i in range(2)]
    w_split = [sb(f"w_split{i}", [P, 2, 3, PIECE], F32R) for i in range(2)]
    h_split = [sb(f"h_split{i}", [P, 2, 2, SPAN], F32R) for i in range(2)]
    th = [sb(f"th{i}", [P, SPAN]) for i in range(2)]
    gated = [sb(f"gated{i}", [P, SPAN]) for i in range(2)]
    hid = [sb(f"hid{i}", [P, SPAN]) for i in range(2)]
    col = [sb(f"col{i}", [P, B]) for i in range(2)]
    top_v = sb("top_v", [P, B, 8])
    top_i = sb("top_i", [P, B, 8], U32)
    top_f = sb("top_f", [P, B, TOP])
    less = sb("less", [P, B, TOP])
    e_top = sb("e_top", [P, B, TOP])
    e_sum = sb("e_sum", [P, B, 1])
    e_rec = sb("e_rec", [P, B, 1])
    w_top = sb("w_top", [P, B, TOP])
    ids = sb("ids", [P, NE, B])
    hit = sb("hit", [P, NE, B])
    term = sb("term", [P, NE, B])
    scale = sb("scale", [P, NCOL, B])
    th_gate = sb("th_gate", [P, B])

    g_ps = [ps(f"g_ps{i}", [P, SPAN]) for i in range(2)]
    u_ps = [ps(f"u_ps{i}", [P, SPAN]) for i in range(2)]
    d_ps = [ps(f"d_ps{i}", [P, D]) for i in range(4)]

    w_loaded = [sem(f"w_loaded{i}") for i in range(2)]
    s_ids, s_route, s_routed, s_etop, s_thg = sem("s_ids"), sem("s_route"), sem("s_routed"), sem("s_etop"), sem("s_thg")
    w_hi_done = sem("w_hi_done")
    w_lo_done = sem("w_lo_done")
    g_done, u_done = sem("g_done"), sem("u_done")
    th_done, gated_done, hid_done, h_hi_done, h_lo_done = (sem(n) for n in ("th_done", "gated_done", "hid_done", "h_hi_done", "h_lo_done"))
    d_done, acc_done = sem("d_done"), sem("acc_done")
    col_done = sem("col_done")
    out_stored = sem("out_stored")

    class Chunk:

        def __init__(self, n, j):
            self.n, self.j = n, j
            self.tiles = 1 if isinstance(n, int) and n == 0 else FE // P
            self.width = self.tiles * P

        def unit(self, t):
            return 4 * self.n + t

        def tile(self, t, f):
            return t if self.tiles == 1 else 2 * self.unit(t) - 4 + f

        def slot(self, t, f):
            return t % 2 if self.tiles == 1 else f

        def before(self, t):
            if t:
                return self, t - 1
            if isinstance(self.n, int):
                return (Chunk(self.n - 1, 1 - self.j), NT - 1) if self.n else None
            return Chunk(self.n - 1, 1 - self.j), NT - 1

        def piece(self, tile, i):
            return tile[:, i, 0:KC * self.width] if i < 2 else tile[:, i, 0:self.tiles * D]

    def chunks(eng, one):
        one(Chunk(0, 0), "shared", 0)
        one(Chunk(1, 1), "shared", HALF)
        with eng.Fori(0, (NSH - 1) // 2) as i:
            for j in range(2):
                one(Chunk(2 * i + 2 + j, j), "shared", (2 * i + 1 + j) * FE + HALF)
        with eng.Fori(0, NE // 2) as i:
            for j in range(2):
                one(Chunk(2 * i + 1 + NSH + j, j), "expert", 2 * i + j)

    def chunks_ahead(eng, one):
        one(Chunk(0, 0), (Chunk(1, 1), 0))
        one(Chunk(1, 1), (Chunk(2, 0), 1))
        with eng.Fori(0, (NCH - 4) // 2) as i:
            for j in range(2):
                one(Chunk(2 * i + 2 + j, j), (Chunk(2 * i + 3 + j, 1 - j), i + 1 + j))
        one(Chunk(NCH - 2, 0), (Chunk(NCH - 1, 1), (NCH - 1) // 2))
        one(Chunk(NCH - 1, 1), None)

    block = whole.enter_context(nc.Block())

    @block.sync
    def _(sp):
        def load(c, kind, at):
            if kind == "shared":
                cols = bass.ds(at, c.width)
                gate, up, down = ws_gate[:, cols], ws_up[:, cols], ws_down[cols, :]
            else:
                gate, up, down = w_gate[at], w_up[at], w_down[at]
            if not (isinstance(c.n, int) and c.n < 2):
                sp.wait_ge(w_lo_done, 3 * c.n - 3)
            for i, src in enumerate((gate, up)):
                sp.dma_start(c.piece(w_raw[c.j], i).rearrange("p (k f) -> p k f", k=KC),
                             src.rearrange("(k p) f -> p k f", p=P)).then_inc(w_loaded[c.j], 16)
            sp.dma_start(c.piece(w_raw[c.j], 2).rearrange("p (k d) -> p k d", d=D),
                         down.rearrange("(k p) d -> p k d", p=P)).then_inc(w_loaded[c.j], 16)

        chunks(sp, load)
        rows = out.rearrange("b p d -> p b d")
        for t in range(NT):
            sp.wait_ge(acc_done, 4 * (4 * (NCH - 1) + t) + 4)
            sp.dma_start(rows[:, t * TT:(t + 1) * TT, :],
                         y_all[:, t * TT * D:(t + 1) * TT * D].rearrange("p (b d) -> p b d", b=TT)).then_inc(out_stored, 16)
        sp.wait_ge(out_stored, 16 * NT)

    @block.gpsimd
    def _(pool):
        pool.iota(ids[:, :, :], pattern=[[1, NE], [0, B]], base=0, channel_multiplier=0,
                  allow_small_or_imprecise_dtypes=True).then_inc(s_ids, 1)

        def lower_half(c, i):
            raw, both = c.piece(w_raw[c.j], i), w_split[c.j]
            hi, lo = c.piece(both[:, 0], i), c.piece(both[:, 1], i)
            pool.wait_ge(w_hi_done, 3 * c.n + i + 1)
            pool.tensor_tensor(lo, raw, hi.bitcast(F32), ALU.subtract).then_inc(w_lo_done, 1)

        def hidden(c, following):
            for t in range(NT):
                for f in range(c.tiles):
                    pool.wait_ge(h_hi_done, c.tile(t, f) + 1)
                    pool.tensor_tensor(h_split[t % 2][:, 1, f, :], hid[c.slot(t, f)][:, :],
                                       h_split[t % 2][:, 0, f, :].bitcast(F32), ALU.subtract).then_inc(h_lo_done, 1)
                if t < 3 and following:
                    lower_half(following[0], t)

        for i in range(3):
            lower_half(Chunk(0, 0), i)
        chunks_ahead(pool, hidden)

    @block.scalar
    def _(act):
        for i in range(3):
            act.wait_ge(w_loaded[0], 48)
            act.activation(Chunk(0, 0).piece(w_split[0][:, 0], i), Chunk(0, 0).piece(w_raw[0], i), ACT.Copy).then_inc(w_hi_done, 1)
        act.wait_ge(s_route, 1)
        act.activation(e_top[:, :, :], less[:, :, :], ACT.Exp).then_inc(s_etop, 1)
        act.activation(th_gate[:, :], logits[:, :, NE], ACT.Tanh, scale=0.5).then_inc(s_thg, 1)

        def upper_half(c, half, i):
            if i == 0:
                act.wait_ge(w_loaded[c.j], 48 * half + 48)
                if not (isinstance(c.n, int) and c.n < 2):
                    act.wait_ge(d_done, 16 * c.n - 16)
            act.activation(c.piece(w_split[c.j][:, 0], i), c.piece(w_raw[c.j], i), ACT.Copy).then_inc(w_hi_done, 1)

        def hidden(c, following):
            for t in range(NT):
                for f in range(c.tiles):
                    y, i = c.tile(t, f), c.slot(t, f)
                    act.wait_ge(g_done, y + 1)
                    if not (isinstance(y, int) and y < 2):
                        act.wait_ge(gated_done, y - 1)
                    act.activation(th[i][:, :], g_ps[i][:, :], ACT.Tanh, scale=0.5).then_inc(th_done, 1)
                    act.wait_ge(hid_done, y + 1)
                    x = c.unit(t)
                    if not (isinstance(x, int) and x < 2):
                        act.wait_ge(d_done, 4 * x - 4)
                    act.activation(h_split[t % 2][:, 0, f, :], hid[i][:, :], ACT.Copy).then_inc(h_hi_done, 1)
                if t < 3 and following:
                    upper_half(*following, t)

        chunks_ahead(act, hidden)

    @block.vector
    def _(dve):
        n_steps = [0]

        def step(ins):
            ins.then_inc(s_routed, 1)
            n_steps[0] += 1
            dve.wait_ge(s_routed, n_steps[0])

        for b in range(B):
            dve.max(top_v[:, b, :], logits[:, b, 0:NE]).then_inc(s_routed, 1)
        n_steps[0] += B
        dve.wait_ge(s_routed, B)
        dve.tensor_tensor(less[:, :, :], top_v[:, :, 0:TOP], top_v[:, :, 0:1].to_broadcast([P, B, TOP]),
                          ALU.subtract).then_inc(s_route, 1)
        for b in range(B):
            dve.max_index(top_i[:, b, :], top_v[:, b, :], logits[:, b, 0:NE]).then_inc(s_routed, 1)
        n_steps[0] += B
        dve.wait_ge(s_routed, 2 * B)
        step(dve.tensor_copy(top_f[:, :, :], top_i[:, :, 0:TOP]))
        dve.wait_ge(s_etop, 1)
        step(dve.tensor_reduce(e_sum[:, :, :].rearrange("p b o -> p (b o)"), e_top[:, :, :], AX_X, ALU.add))
        step(dve.reciprocal(e_rec[:, :, :], e_sum[:, :, :]))
        step(dve.tensor_scalar(e_rec[:, :, :], e_rec[:, :, :], tanh_g[:, 1:2], None, ALU.mult))
        step(dve.tensor_tensor(w_top[:, :, :], e_top[:, :, :], e_rec[:, :, :].to_broadcast([P, B, TOP]), ALU.mult))
        dve.wait_ge(s_ids, 1)
        for k in range(TOP):
            across = lambda t: t[:, :, k:k + 1].rearrange("p b o -> p o b").to_broadcast([P, NE, B])
            step(dve.tensor_tensor(hit[:, :, :], ids[:, :, :], across(top_f), ALU.is_equal))
            if k == 0:
                step(dve.tensor_tensor(scale[:, 0:NE, :], hit[:, :, :], across(w_top), ALU.mult))
            else:
                step(dve.tensor_tensor(term[:, :, :], hit[:, :, :], across(w_top), ALU.mult))
                step(dve.tensor_tensor(scale[:, 0:NE, :], scale[:, 0:NE, :], term[:, :, :], ALU.add))
        dve.wait_ge(s_thg, 1)
        step(dve.tensor_scalar(th_gate[:, :], th_gate[:, :], 0.5, 0.5, ALU.mult, ALU.add))
        step(dve.tensor_scalar(scale[:, NE, :], th_gate[:, :], tanh_g[:, 1:2], None, ALU.mult))

        def accumulate(c, t):
            x = c.unit(t)
            for i in range(TT):
                dve.wait_ge(d_done, 4 * x + i + 1)
                if i == 0 and t == 0:
                    dve.wait_ge(col_done, c.n + 1)
                if not (isinstance(x, int) and x < 4):
                    dve.wait_ge(acc_done, 4 * x + i - 15)
                y_b = y_all[:, (t * TT + i) * D:(t * TT + i + 1) * D]
                dve.scalar_tensor_tensor(out=y_b, in0=d_ps[i][:, :], scalar=col[c.j][:, t * TT + i:t * TT + i + 1],
                                         in1=y_b, op0=ALU.mult, op1=ALU.add).then_inc(acc_done, 1)

        def hidden(c, kind, at):
            src = scale[:, NE, :] if kind == "shared" else scale[:, bass.ds(at, 1), :].rearrange("p o b -> p (o b)")
            for t in range(NT):
                for f in range(c.tiles):
                    y, i = c.tile(t, f), c.slot(t, f)
                    dve.wait_ge(th_done, y + 1)
                    dve.scalar_tensor_tensor(out=gated[i][:, :], in0=th[i][:, :], scalar=1.0, in1=g_ps[i][:, :],
                                             op0=ALU.add, op1=ALU.mult).then_inc(gated_done, 1)
                    dve.wait_ge(gated_done, y + 1)
                    dve.wait_ge(u_done, y + 1)
                    if not (isinstance(y, int) and y < 2):
                        dve.wait_ge(h_lo_done, y - 1)
                    dve.scalar_tensor_tensor(out=hid[i][:, :], in0=gated[i][:, :], scalar=0.5, in1=u_ps[i][:, :],
                                             op0=ALU.mult, op1=ALU.mult).then_inc(hid_done, 1)
                if c.before(t):
                    accumulate(*c.before(t))
                if t == 0:
                    dve.tensor_copy(col[c.j][:, :], src).then_inc(col_done, 1)

        chunks(dve, hidden)
        accumulate(Chunk(NCH - 1, 1), NT - 1)

    @block.tensor
    def _(pe):
        TERMS = ((0, 0), (1, 0), (0, 1))

        def first_products(c, t, f):
            y, i = c.tile(t, f), c.slot(t, f)
            if t == 0 and f == 0:
                pe.wait_ge(w_lo_done, 3 * c.n + 2)
            if not (isinstance(y, int) and y < 2):
                pe.wait_ge(hid_done, y - 1)
            for piece, (dst, done) in enumerate(((g_ps, g_done), (u_ps, u_done))):
                n = 0
                for k in range(KC):
                    for a, b in TERMS:
                        w = c.piece(w_split[c.j][:, a], piece).rearrange("p (k f) -> p k f", k=KC)
                        mm = pe.matmul(dst[i][:, :], w[:, k, f * P:(f + 1) * P], yn_t[:, b, k, t * SPAN:(t + 1) * SPAN],
                                       start=(n == 0), stop=(n == 3 * KC - 1))
                        n += 1
                mm.then_inc(done, 1)

        def down(c, t):
            x = c.unit(t)
            if t == 0:
                pe.wait_ge(w_lo_done, 3 * c.n + 3)
            pe.wait_ge(h_lo_done, c.tile(t, c.tiles - 1) + 1)
            for i in range(TT):
                if not (isinstance(x, int) and x < 1):
                    pe.wait_ge(acc_done, 4 * x + i - 3)
                n = 0
                for f in range(c.tiles):
                    for a, b in TERMS:
                        w = c.piece(w_split[c.j][:, b], 2).rearrange("p (k d) -> p k d", d=D)
                        mm = pe.matmul(d_ps[i][:, :], h_split[t % 2][:, a, f, i * P:(i + 1) * P], w[:, f, :],
                                       start=(n == 0), stop=(n == 3 * c.tiles - 1))
                        n += 1
                mm.then_inc(d_done, 1)

        def chunk(c, kind, at):
            for t in range(NT):
                for f in range(c.tiles):
                    first_products(c, t, f)
                if c.before(t):
                    down(*c.before(t))

        chunks(pe, chunk)
        down(Chunk(NCH - 1, 1), NT - 1)


_INS = ['x', 'ctx_2048', 'g_xattn', 'g_ffn', 'L0_ffn_w_router', 'L0_ffn_w_gate', 'L0_ffn_w_up', 'L0_ffn_w_down',
        'L0_ffn_w_sh_gate', 'L0_ffn_w_sh_up', 'L0_ffn_w_sh_down', 'L0_ffn_w_sh_expert_gate']


def kernel(**inputs):
    import numpy as _np
    import concourse.bacc as _bacc
    from concourse import mybir as _mybir
    from concourse.bass_utils import run_bass_kernel_spmd as _run

    nc = _bacc.Bacc("TRN2", target_bir_lowering=False, num_devices=1)
    arrays, args = {}, []
    for name in _INS:
        a = _np.ascontiguousarray(inputs[name])
        arrays[f"in_{name}_dram"] = a
        args.append(nc.dram_tensor(f"in_{name}_dram", a.shape, _mybir.dt.from_np(a.dtype), kind="ExternalInput").ap())
    shape = tuple(inputs['x'].shape)
    args.append(nc.dram_tensor("out_0_dram", shape, _mybir.dt.float32, kind="ExternalOutput").ap())
    gated_block(nc, *args)
    r = _run(nc, [arrays], core_ids=[0])
    return r.results[0]["out_0_dram"]
```

```python
from contextlib import ExitStack

import concourse.bass as bass
from concourse import mybir

F32 = mybir.dt.float32
F32R = mybir.dt.float32r
U32 = mybir.dt.uint32
ALU = mybir.AluOpType
ACT = mybir.ActivationFunctionType
AX_X = mybir.AxisListType.X
P = 128


class Group:

    def __init__(self, q, r):
        self.q, self.r, self.g = q, r, 4 * r + q

    def known(self):
        return isinstance(self.r, int)

    def at_least(self, n):
        return not self.known() or self.g >= n

    def before(self, n):
        return not self.known() or self.g < n


class Chunk:

    def __init__(self, n, j, ex):
        self.n, self.j, self.ex = n, j, ex
        self.tiles = 1 if isinstance(n, int) and n == 0 else ex.FE // P
        self.width = self.tiles * P

    def unit(self, t):
        return 4 * self.n + t

    def tile(self, t, f):
        return t if self.tiles == 1 else 2 * self.unit(t) - 4 + f

    def slot(self, t, f):
        return t % 2 if self.tiles == 1 else f

    def before(self, t):
        if t:
            return self, t - 1
        if isinstance(self.n, int) and self.n == 0:
            return None
        return Chunk(self.n - 1, 1 - self.j, self.ex), self.ex.NT - 1

    def piece(self, tile, i):
        return tile[:, i, 0:self.ex.KC * self.width] if i < 2 else tile[:, i, 0:self.tiles * self.ex.D]


class Experts:
    TERMS = ((0, 0), (1, 0), (0, 1))

    def __init__(self, sem, yn_t, ws, we, w_raw, w_split, g_ps, u_ps):
        self.NE, self.D, self.FE = we[0].shape
        self.FS = ws[0].shape[1]
        self.KC = self.D // P
        self.SPAN = 512
        self.NT = yn_t.shape[3] // self.SPAN
        self.HALF = self.FS % self.FE
        self.yn_t, self.ws, self.we = yn_t, ws, we
        self.w_raw, self.w_split, self.g_ps, self.u_ps = w_raw, w_split, g_ps, u_ps
        self.w_loaded = [sem(f"w_loaded{i}") for i in range(2)]
        self.w_hi_done = sem("w_hi_done")
        self.w_lo_done = sem("w_lo_done")
        self.g_done, self.u_done = sem("g_done"), sem("u_done")

    def load_weights(self, sp, c, kind, at):
        if kind == "shared":
            cols = bass.ds(at, c.width)
            gate, up, down = self.ws[0][:, cols], self.ws[1][:, cols], self.ws[2][cols, :]
        else:
            gate, up, down = (w[at] for w in self.we)
        if not (isinstance(c.n, int) and c.n < 2):
            sp.wait_ge(self.w_lo_done, 3 * c.n - 3)
        for i, src in enumerate((gate, up)):
            sp.dma_start(c.piece(self.w_raw[c.j], i).rearrange("p (k f) -> p k f", k=self.KC),
                         src.rearrange("(k p) f -> p k f", p=P)).then_inc(self.w_loaded[c.j], 16)
        sp.dma_start(c.piece(self.w_raw[c.j], 2).rearrange("p (k d) -> p k d", d=self.D),
                     down.rearrange("(k p) d -> p k d", p=P)).then_inc(self.w_loaded[c.j], 16)

    def upper_weights(self, act, c, i):
        act.activation(c.piece(self.w_split[c.j][:, 0], i), c.piece(self.w_raw[c.j], i), ACT.Copy).then_inc(self.w_hi_done, 1)

    def lower_weights(self, pool, c, i):
        hi, lo = (c.piece(self.w_split[c.j][:, a], i) for a in range(2))
        pool.wait_ge(self.w_hi_done, 3 * c.n + i + 1)
        pool.tensor_tensor(lo, c.piece(self.w_raw[c.j], i), hi.bitcast(F32), ALU.subtract).then_inc(self.w_lo_done, 1)

    def first_products(self, pe, c, t, f, piece):
        i = c.slot(t, f)
        dst, done = ((self.g_ps, self.g_done), (self.u_ps, self.u_done))[piece]
        n = 0
        for k in range(self.KC):
            for a, b in self.TERMS:
                w = c.piece(self.w_split[c.j][:, a], piece).rearrange("p (k f) -> p k f", k=self.KC)
                mm = pe.matmul(dst[i], w[:, k, f * P:(f + 1) * P], self.yn_t[:, b, k, t * self.SPAN:(t + 1) * self.SPAN],
                               start=(n == 0), stop=(n == 3 * self.KC - 1))
                n += 1
        mm.then_inc(done, 1)


def gated_block(nc, x, ctx_in, g_xattn, g_ffn, w_router, w_gate, w_up, w_down, ws_gate, ws_up, ws_down, w_eg, out):
    B, TOK, D = x.shape
    NE, _, FE = w_gate.shape
    FS = ws_gate.shape[1]
    HEADS = 8
    HD = TOK // HEADS
    HG = 4
    GR = HG * HD
    NG = B * HEADS // HG
    KC = D // P
    SCALE = float(HD) ** -0.5
    EPS = 1e-5
    PAD = 96
    TOP = 4
    NCOL = NE + 1
    assert TOK == P and D == 512 and KC == 4 and HG * 32 == P and NG == 32 and FE == 256 and TOP == KC

    with ExitStack() as whole:
        def sem(name):
            return whole.enter_context(nc.semaphore(name))

        def held(stack, name, shape, dt=F32):
            return stack.enter_context(nc.sbuf_tensor(name, shape, dt))

        y_all = held(whole, "y_all", [P, B * D])
        yn_t = held(whole, "yn_t", [P, 2, KC, B * TOK], F32R)
        ident = held(whole, "ident", [P, P])
        w_r = held(whole, "w_r", [P, KC, 32])
        tanh_g = held(whole, "tanh_g", [P, 2])
        with ExitStack() as place_of_weights:
            xn = [held(place_of_weights, f"xn{i}", [P, KC, TOK]) for i in range(2)]
            early_stacks = [held(place_of_weights, f"stack{i}", [P, HG, D], F32R) for i in range(4)]
        w_raw = held(whole, "w_raw0", [P, 3, KC * FE])
        w_split = held(whole, "w_split0", [P, 2, 3, KC * FE], F32R)
        score_ps = whole.enter_context(nc.psum_tensor("score_ps", [P, 2, 2, D], F32))

        attn = ExitStack()
        whole.enter_context(attn)
        sb = lambda name, shape, dt=F32: held(attn, name, shape, dt)
        ps = lambda name, shape, dt=F32: attn.enter_context(nc.psum_tensor(name, shape, dt))

        q_stack = early_stacks[0::2] + [sb(f"q_stack{i}", [P, HG, D], F32R) for i in (2, 3)]
        k_stack = early_stacks[1::2] + [sb(f"k_stack{i}", [P, HG, D], F32R) for i in (2, 3)]
        probs = sb("probs", [P, 2, HG, D])
        v_rows = [sb(f"v_rows{i}", [GR, D]) for i in range(2)]
        v_t = [sb(f"v_t{i}", [P, KC, HG, 32]) for i in range(2)]
        maxima = [sb(f"maxima{i}", [P, 4 * HG]) for i in range(2)]
        max_hi = sb("max_hi", [4 * HG, P], F32R)
        max_lo = sb("max_lo", [4 * HG, P], F32R)
        o_sb = sb("o_sb", [P, D])
        recip = sb("recip", [P, KC, HG, 1])
        attn_t = sb("attn_t", [P, KC, TOK])
        x_res = [sb(f"x_res{i}", [P, D]) for i in range(2)]
        yn = sb("yn", [P, D])
        yn32 = sb("yn32", [P, KC, TOK])
        expo = sb("expo", [P, 1])
        g_raw = sb("g_raw", [P, 2])
        bn = sb("bn", [P, 2, 6])
        mean_var = [sb(f"mean_var{i}", [P, 2]) for i in range(2)]
        var_eps = [sb(f"var_eps{i}", [P, 1]) for i in range(2)]
        rstd = [sb(f"rstd{i}", [P, 1]) for i in range(2)]
        bn2 = sb("bn2", [P, 6])
        mean_var2 = sb("mean_var2", [P, 2])
        var_eps2 = sb("var_eps2", [P, 1])
        rstd2 = sb("rstd2", [P, 1])

        x_in, k_in = ([y_all[:, b * D:(b + 1) * D] for b in (B - n, B - n + 1)] for n in (2, 4))
        place = lambda a, b: yn_t[:, a, :, b * TOK:(b + 1) * TOK]
        q_hi, k_hi = ([place(0, b) for b in (B - n, B - n + 1)] for n in (2, 4))
        q_lo, k_lo = ([place(1, b) for b in (B - n, B - n + 1)] for n in (2, 4))
        in_chunks = lambda tile: tile.rearrange("p (k t) -> p k t", k=KC)
        flat = lambda tile: tile[:, :, :].rearrange("p k t -> p (k t)")

        ex = Experts(sem, yn_t, (ws_gate, ws_up, ws_down), (w_gate, w_up, w_down),
                     w_raw=[w_raw], w_split=[w_split],
                     g_ps=[score_ps[:, i, 0, :] for i in range(2)], u_ps=[score_ps[:, i, 1, :] for i in range(2)])
        first_chunk = Chunk(0, 0, ex)

        sa_ps = score_ps
        sb_ps = ps("sb_ps", [P, 2, D])
        o_ps = ps("o_ps", [P, D])
        m_ps = ps("m_ps", [P, D])

        halves = {n: nc.dram_tensor(f"{n}_dram", (B, HEADS, HD, D), F32, kind="Internal").ap()
                  for n in ("q_hi", "q_lo", "k_hi", "k_lo")}

        s_const, s_small, s_tanh = sem("s_const"), sem("s_small"), sem("s_tanh")
        fixed_rows = [sem(f"fixed_rows{i}") for i in range(4)]
        x_loaded = [sem(f"x_loaded{i}") for i in range(2)]
        k_loaded = [sem(f"k_loaded{i}") for i in range(2)]
        k_stored = [sem(f"k_stored{i}") for i in range(2)]
        q_stored = [sem(f"q_stored{i}") for i in range(2)]
        bn_done, mv_done, ve_done, rstd_done, xn_done = (sem(n) for n in ("bn_done", "mv_done", "ve_done", "rstd_done", "xn_done"))
        q_hi_done, q_lo_done, k_hi_done, k_lo_done = (sem(n) for n in ("q_hi_done", "q_lo_done", "k_hi_done", "k_lo_done"))
        stack_loaded = [sem(f"stack_loaded{i}") for i in range(4)]
        max_rows = [sem(f"max_rows{i}") for i in range(4)]
        v_loaded = [sem(f"v_loaded{i}") for i in range(2)]
        res_loaded = [sem(f"res_loaded{i}") for i in range(2)]
        y_kept = [sem(f"y_kept{i}") for i in range(2)]
        sa_done = sem("sa_done")
        max_done = sem("max_done")
        vm_done = sem("vm_done")
        mhi_done, mlo_done, vt_done = sem("mhi_done"), sem("mlo_done"), sem("vt_done")
        sb_done = sem("sb_done")
        exp_done = sem("exp_done")
        pv_done = sem("pv_done")
        o_done = sem("o_done")
        ot_done, rc_done, norm_done = sem("ot_done"), sem("rc_done"), sem("norm_done")
        back_done, y_done = sem("back_done"), sem("y_done")
        bn2_done, mv2_done, ve2_done, rstd2_done, yn_done = (sem(n) for n in ("bn2_done", "mv2_done", "ve2_done", "rstd2_done", "yn_done"))
        ynt_done, yn32_done, ynhi_done, ynlo_done = (sem(n) for n in ("ynt_done", "yn32_done", "ynhi_done", "ynlo_done"))

        def batch_back(s):
            return 2 * s.r - 1 if s.q == 0 else 2 * s.r

        def batch_late(s):
            return 2 * s.r - 1 if s.q == 1 else 2 * s.r

        def has_back(s):
            return s.q % 2 == 0 and s.at_least(2)

        def has_late(s):
            return s.q % 2 == 1 and s.at_least(3)

        def prepared(s):
            return s.q % 2 == 0 and s.before(NG - 4)

        def slots(eng, slot):
            for g in range(7):
                slot(Group(g % 4, g // 4))
            with eng.Fori(1, 6) as i:
                for q in (3, 4, 5, 6):
                    slot(Group(q % 4, i + q // 4))
            for g in range(27, NG):
                slot(Group(g % 4, g // 4))

        def fix_rows(eng, stack, i):
            if stack is q_stack:
                eng.memset(stack[i][0:PAD, :, :].bitcast(F32), 0.0).then_inc(fixed_rows[i], 1)
            else:
                eng.memset(stack[i][0:PAD + 2, :, :].bitcast(F32), -1.0).then_inc(fixed_rows[i], 1)

        block = attn.enter_context(nc.Block())

        @block.sync
        def _(sp):
            def load_rows(b, j, waits):
                if waits:
                    sp.wait_ge(xn_done, b - 1)
                    sp.wait_ge(k_lo_done, b - 1)
                sp.dma_start(x_in[j], x[b]).then_inc(x_loaded[j], 16)
                sp.dma_start(k_in[j], ctx_in[b]).then_inc(k_loaded[j], 16)

            def store_halves(b, j):
                for name, tile, done, stored in (("k_hi", k_hi, k_hi_done, k_stored), ("k_lo", k_lo, k_lo_done, k_stored),
                                                 ("q_hi", q_hi, q_hi_done, q_stored), ("q_lo", q_lo, q_lo_done, q_stored)):
                    sp.wait_ge(done, b + 1)
                    sp.dma_start(halves[name][b].rearrange("h e (k t) -> (h e) k t", k=KC),
                                 tile[j].bitcast(F32)).then_inc(stored[j], 16)

            def load_values(j, b, half):
                sp.dma_start(v_rows[j][:, :], ctx_in[b][half * GR:(half + 1) * GR, :]).then_inc(v_loaded[j], 16)

            def load_stack(i, b, half, n):
                for stack, stored, names in ((k_stack, k_stored, ("k_hi", "k_lo", "k_hi")), (q_stack, q_stored, ("q_hi", "q_hi", "q_lo"))):
                    sp.wait_ge(stored[half_of_pair(i)], 32 * n + 32)
                    for m, name in enumerate(names):
                        src = halves[name][b][half * HG:(half + 1) * HG].rearrange("h e d -> e h d")
                        sp.dma_start(stack[i][m * HD:(m + 1) * HD, :, :].bitcast(F32), src).then_inc(stack_loaded[i], 16)

            def half_of_pair(i):
                return i // 2

            def store_max_rows(i, g):
                sp.wait_ge(mhi_done, g + 1)
                sp.dma_start(q_stack[i][PAD:PAD + 1, :, :].bitcast(F32), max_hi[:, :].bitcast(F32)).then_inc(max_rows[i], 16)
                sp.wait_ge(mlo_done, g + 1)
                sp.dma_start(q_stack[i][PAD + 1:PAD + 2, :, :].bitcast(F32), max_lo[:, :].bitcast(F32)).then_inc(max_rows[i], 16)

            for b in range(2):
                load_rows(b, b, False)
            for b in range(2):
                store_halves(b, b)
                for half in range(2):
                    sp.wait_ge(fixed_rows[2 * b + half], 2)
                    load_stack(2 * b + half, b, half, 0)
                if b == 0:
                    load_values(0, 0, 0)
                    load_values(1, 0, 1)
            load_rows(2, 0, True)
            store_max_rows(0, 0)

            def keep_y(b, j):
                sp.wait_ge(yn_done, b + 1)
                sp.dma_start(y_all[:, bass.ds(b * D, D)], x_res[j][:, :]).then_inc(y_kept[j], 16)

            def slot(s):
                if s.before(NG - 2):
                    sp.wait_ge(vm_done, s.g + 1)
                    load_values(s.q % 2, 2 * s.r + s.q // 2 + 1, s.q % 2)
                if s.q % 2 == 0:
                    b, j = 2 * s.r + s.q // 2, s.q // 2
                    if s.at_least(4):
                        keep_y(b - 2, j)
                        sp.wait_ge(y_kept[j], 16 * s.r)
                    sp.dma_start(x_res[j][:, :], x[b]).then_inc(res_loaded[j], 16)
                if s.before(NG - 1):
                    store_max_rows((s.q + 1) % 4, s.g + 1)
                if prepared(s):
                    store_halves(2 * s.r + 2 + s.q // 2, s.q // 2)
                if s.q % 2 == 1 and s.before(NG - 5):
                    load_rows(2 * s.r + 3 + s.q // 2, (s.q // 2 + 1) % 2, True)
                if s.before(NG - 4):
                    sp.wait_ge(sb_done, 16 * s.g + 16)
                    load_stack(s.q, 2 * s.r + 2 + s.q // 2, s.q % 2, s.r + 1)

            slots(sp, slot)
            sp.wait_ge(sb_done, 16 * (NG - 2))
            ex.load_weights(sp, first_chunk, "shared", 0)
            for j in range(2):
                keep_y(B - 2 + j, j)
            for j in range(2):
                sp.wait_ge(y_kept[j], 16 * (B // 2))

        @block.gpsimd
        def _(pool):
            def lower_keys(b, j):
                pool.wait_ge(k_hi_done, b + 1)
                pool.tensor_tensor(k_lo[j], in_chunks(k_in[j]), k_hi[j].bitcast(F32), ALU.subtract).then_inc(k_lo_done, 1)

            def deviation(b, j):
                pool.wait_ge(ve_done, b + 1)
                pool.tensor_tensor(rstd[j][:, :], var_eps[j][:, :], expo[:, :], ALU.pow).then_inc(rstd_done, 1)

            def prepare(b, j, n):
                pool.wait_ge(k_loaded[j], 16 * n + 16)
                pool.wait_ge(k_stored[j], 32 * n)
                deviation(b, j)
                pool.tensor_copy(k_hi[j], in_chunks(k_in[j])).then_inc(k_hi_done, 1)
                pool.wait_ge(rstd_done, b + 1)
                lower_keys(b, j)
                pool.tensor_scalar(flat(xn[j]), x_in[j], mean_var[j][:, 0:1], rstd[j][:, 0:1],
                                   ALU.subtract, ALU.mult).then_inc(xn_done, 1)
                lower_queries(b, j)

            def lower_queries(b, j):
                pool.wait_ge(q_hi_done, b + 1)
                pool.tensor_tensor(q_lo[j], xn[j][:, :, :], q_hi[j].bitcast(F32), ALU.subtract).then_inc(q_lo_done, 1)

            pool.memset(ident[:, :], 0.0).then_inc(s_const, 1)
            pool.memset(expo[:, :], -0.5).then_inc(s_const, 1)
            pool.memset(w_r[:, :, :], 0.0).then_inc(s_const, 1)
            fix_rows(pool, q_stack, 0)
            fix_rows(pool, k_stack, 0)
            pool.wait_ge(s_const, 3)
            deviation(0, 0)
            lower_keys(0, 0)
            pool.affine_select(out=ident[:, :], in_=ident[:, :], compare_op=ALU.not_equal, fill=1.0,
                               base=0, pattern=[[-1, P]], channel_multiplier=1).then_inc(s_const, 1)
            for j in range(2):
                pool.memset(v_t[j][:, :, :, :], 0.0).then_inc(s_const, 1)
            pool.wait_ge(s_const, 6)
            for j in range(2):
                pool.memset(v_t[j][:, :, :, HD:HD + 1], 1.0).then_inc(s_const, 1)
            deviation(1, 1)
            lower_keys(1, 1)
            for stack, i in ((q_stack, 2), (k_stack, 2), (q_stack, 3)):
                fix_rows(pool, stack, i)

            def reciprocal_deviation(b):
                pool.wait_ge(ve2_done, b + 1)
                pool.tensor_tensor(rstd2[:, :], var_eps2[:, :], expo[:, :], ALU.pow).then_inc(rstd2_done, 1)

            def split_yn(b):
                at = bass.ds(b * TOK, TOK)
                pool.wait_ge(ynhi_done, b + 1)
                pool.tensor_tensor(yn_t[:, 1, :, at], yn32[:, :, :], yn_t[:, 0, :, at].bitcast(F32),
                                   ALU.subtract).then_inc(ynlo_done, 1)

            def slot(s):
                if prepared(s):
                    prepare(2 * s.r + 2 + s.q // 2, s.q // 2, s.r + 1)
                if has_late(s):
                    reciprocal_deviation(batch_late(s))
                    split_yn(batch_late(s))

            slots(pool, slot)
            for i in range(3):
                ex.lower_weights(pool, first_chunk, i)
            reciprocal_deviation(B - 1)
            split_yn(B - 1)

        @block.scalar
        def _(act):
            act.wait_ge(k_loaded[0], 16)
            act.activation(k_hi[0], in_chunks(k_in[0]), ACT.Copy).then_inc(k_hi_done, 1)

            def upper_queries(b, j, n):
                act.wait_ge(xn_done, b + 1)
                if not (isinstance(n, int) and n == 0):
                    act.wait_ge(q_stored[j], 32 * n)
                act.activation(q_hi[j], xn[j][:, :, :], ACT.Copy).then_inc(q_hi_done, 1)

            upper_queries(0, 0, 0)
            act.wait_ge(k_loaded[1], 16)
            act.activation(k_hi[1], in_chunks(k_in[1]), ACT.Copy).then_inc(k_hi_done, 1)
            upper_queries(1, 1, 0)
            act.wait_ge(s_const, 3)
            act.dma_start(w_r[:, :, 0:NE], w_router.rearrange("(k p) e -> p k e", p=P)).then_inc(s_small, 16)
            act.dma_start(w_r[:, :, NE:NCOL], w_eg.rearrange("(k p) e -> p k e", p=P),
                          allow_slow_non_contiguous=True).then_inc(s_small, 16)
            act.dma_start(g_raw[:, 0:1], g_xattn.partition_broadcast(P)).then_inc(s_small, 16)
            act.dma_start(g_raw[:, 1:2], g_ffn.partition_broadcast(P)).then_inc(s_small, 16)
            act.wait_ge(s_small, 64)
            act.activation(tanh_g[:, :], g_raw[:, :], ACT.Tanh).then_inc(s_tanh, 1)

            def copy_out(g):
                act.wait_ge(pv_done, 4 * g + 4)
                if not (isinstance(g, int) and g == 0):
                    act.wait_ge(ot_done, g)
                act.activation(o_sb[:, :], o_ps[:, :], ACT.Copy).then_inc(o_done, 1)

            def copy_yn(b):
                act.wait_ge(ynt_done, b + 1)
                if not (isinstance(b, int) and b == 0):
                    act.wait_ge(ynhi_done, b)
                    act.wait_ge(ynlo_done, b)
                act.activation(yn32[:, :, :].rearrange("p k t -> p (k t)"), m_ps[:, :], ACT.Copy).then_inc(yn32_done, 1)

            def slot(s):
                for c in range(KC):
                    if c == 2 and has_late(s):
                        copy_yn(batch_late(s))
                    if c == 3 and prepared(s):
                        upper_queries(2 * s.r + 2 + s.q // 2, s.q // 2, s.r + 1)
                    for j in range(HG):
                        n = 16 * s.g + HG * c + j
                        act.wait_ge(sb_done, n + 1)
                        if j == 0 and (c >= 2 or s.at_least(1)):
                            act.wait_ge(pv_done, 4 * s.g + c - 1)
                        act.activation(probs[:, c % 2, j, :], sb_ps[:, j % 2, :], ACT.Exp, scale=SCALE).then_inc(exp_done, 1)
                    if c == 0 and s.at_least(1):
                        copy_out(s.g - 1)

            slots(act, slot)
            act.wait_ge(ex.w_loaded[0], 48)
            for i in range(2):
                ex.upper_weights(act, first_chunk, i)
            copy_out(NG - 1)
            ex.upper_weights(act, first_chunk, 2)
            copy_yn(B - 1)

        @block.vector
        def _(dve):
            def statistics(j, n):
                dve.wait_ge(x_loaded[j], 16 * n + 16)
                dve.bn_stats(bn[:, j, :], x_in[j]).then_inc(bn_done, 1)

            def first_variance(b, j):
                dve.bn_aggr(mean_var[j][:, :], bn[:, j, :]).then_inc(mv_done, 1)
                dve.wait_ge(mv_done, b + 1)
                dve.tensor_scalar(var_eps[j][:, :], mean_var[j][:, 1:2], EPS, None, ALU.add).then_inc(ve_done, 1)

            fix_rows(dve, q_stack, 1)
            for j in range(2):
                statistics(j, 0)
                dve.wait_ge(bn_done, j + 1)
                first_variance(j, j)
                dve.wait_ge(rstd_done, j + 1)
                dve.tensor_scalar(flat(xn[j]), x_in[j], mean_var[j][:, 0:1], rstd[j][:, 0:1],
                                  ALU.subtract, ALU.mult).then_inc(xn_done, 1)
                dve.wait_ge(q_hi_done, j + 1)
                dve.tensor_tensor(q_lo[j], xn[j][:, :, :], q_hi[j].bitcast(F32), ALU.subtract).then_inc(q_lo_done, 1)
                if j == 0:
                    fix_rows(dve, k_stack, 1)
            fix_rows(dve, k_stack, 3)
            dve.wait_ge(s_const, 8)
            dve.wait_ge(s_tanh, 1)

            def unit(q, g, u):
                n = 8 * g + u
                dve.wait_ge(sa_done, n + 1)
                if u == 0 and not (isinstance(g, int) and g < 2):
                    dve.wait_ge(vm_done, g - 1)
                dve.tensor_reduce(maxima[q % 2][:, 2 * u:2 * u + 2], sa_ps[:, u % 2, :, :], AX_X, ALU.max).then_inc(max_done, 1)

            def values_and_maxima(q, g, n):
                dve.wait_ge(vm_done, g + 1)
                if not (isinstance(g, int) and g == 0):
                    rows = max_rows[(q - 1) % 4]
                    dve.wait_ge(rows, 32 * n + 32)
                dve.tensor_copy(max_hi[:, :], m_ps[0:4 * HG, 256:384]).then_inc(mhi_done, 1)
                dve.wait_ge(mhi_done, g + 1)
                dve.tensor_tensor(max_lo[:, :], m_ps[0:4 * HG, 256:384], max_hi[:, :].bitcast(F32), ALU.subtract).then_inc(mlo_done, 1)
                if not (isinstance(g, int) and g < 2):
                    dve.wait_ge(pv_done, 4 * g - 4)
                dve.tensor_copy(v_t[q % 2][:, :, :, 0:HD],
                                m_ps[:, 0:KC * GR].rearrange("p (k h e) -> p k h e", k=KC, h=HG)).then_inc(vt_done, 1)

            def normalise(q, g, b):
                view = m_ps[:, :].rearrange("p (k h e) -> p k h e", k=KC, h=HG)
                dve.wait_ge(ot_done, g + 1)
                dve.reciprocal(recip[:, :, :, :], view[:, :, :, HD:HD + 1]).then_inc(rc_done, 1)
                if q % 2 == 0 and not (isinstance(g, int) and g == 0):
                    dve.wait_ge(back_done, b)
                dve.wait_ge(rc_done, g + 1)
                dst = attn_t[:, :, (q % 2) * GR:(q % 2 + 1) * GR].rearrange("p k (h e) -> p k h e", h=HG)
                dve.tensor_tensor(dst, view[:, :, :, 0:HD], recip[:, :, :, :].to_broadcast([P, KC, HG, HD]),
                                  ALU.mult).then_inc(norm_done, 1)

            def residual(b, j, n):
                dve.wait_ge(back_done, b + 1)
                dve.wait_ge(res_loaded[j], 16 * n + 16)
                dve.scalar_tensor_tensor(out=x_res[j][:, :], in0=m_ps[:, :], scalar=tanh_g[:, 0:1], in1=x_res[j][:, :],
                                         op0=ALU.mult, op1=ALU.add).then_inc(y_done, 1)
                dve.wait_ge(y_done, b + 1)
                dve.bn_stats(bn2[:, :], x_res[j][:, :]).then_inc(bn2_done, 1)

            def variance(b):
                dve.bn_aggr(mean_var2[:, :], bn2[:, :]).then_inc(mv2_done, 1)
                dve.wait_ge(mv2_done, b + 1)
                dve.tensor_scalar(var_eps2[:, :], mean_var2[:, 1:2], EPS, None, ALU.add).then_inc(ve2_done, 1)

            def normed(b, j):
                dve.wait_ge(rstd2_done, b + 1)
                if not (isinstance(b, int) and b == 0):
                    dve.wait_ge(ynt_done, b)
                dve.tensor_scalar(yn[:, :], x_res[j][:, :], mean_var2[:, 0:1], rstd2[:, 0:1],
                                  ALU.subtract, ALU.mult).then_inc(yn_done, 1)

            def upper_half(b):
                dve.wait_ge(yn32_done, b + 1)
                dve.tensor_scalar(yn_t[:, 0, :, bass.ds(b * TOK, TOK)], yn32[:, :, :], 1.0, None, ALU.mult).then_inc(ynhi_done, 1)

            def batch_of_previous(s):
                return 2 * s.r + (s.q + 1) // 2 - 1

            def slot(s):
                q, g = s.q, s.g
                q1, q2 = (q + 1) % 4, (q + 2) % 4
                if has_late(s):
                    residual(batch_late(s), 1 if q == 1 else 0, s.r - 1 if q == 1 else s.r)
                    dve.wait_ge(bn2_done, batch_late(s) + 1)
                if prepared(s):
                    statistics(q // 2, s.r + 1)
                    dve.wait_ge(bn_done, 2 * s.r + q // 2 + 3)
                if s.before(NG - 1):
                    unit(q1, g + 1, 4)
                if prepared(s):
                    first_variance(2 * s.r + q // 2 + 2, q // 2)
                if has_late(s):
                    variance(batch_late(s))
                if s.before(NG - 1):
                    unit(q1, g + 1, 5)
                if has_late(s):
                    normed(batch_late(s), 1 if q == 1 else 0)
                    normalise((q - 1) % 4, g - 1, batch_of_previous(s))
                if s.before(NG - 1):
                    unit(q1, g + 1, 6)
                if s.at_least(1) and not has_late(s):
                    normalise((q - 1) % 4, g - 1, batch_of_previous(s))
                if s.before(NG - 1):
                    unit(q1, g + 1, 7)
                if s.before(NG - 2):
                    unit(q2, g + 2, 0)
                if s.before(NG - 1):
                    values_and_maxima(q1, g + 1, s.r)
                if s.before(NG - 2):
                    unit(q2, g + 2, 1)
                    unit(q2, g + 2, 2)
                if has_late(s):
                    upper_half(batch_late(s))
                if s.before(NG - 2):
                    unit(q2, g + 2, 3)

            for u in range(8):
                unit(0, 0, u)
            unit(1, 1, 0)
            unit(1, 1, 1)
            values_and_maxima(0, 0, None)
            unit(1, 1, 2)
            unit(1, 1, 3)
            slots(dve, slot)
            normalise(3, NG - 1, B - 1)
            residual(B - 1, 1, B // 2 - 1)
            dve.wait_ge(bn2_done, B)
            variance(B - 1)
            normed(B - 1, 1)
            upper_half(B - 1)

        @block.tensor
        def _(pe):
            pe.wait_ge(s_const, 8)

            def scores(i, g, r, u, half):
                n = 8 * g + u
                if u == 0 and half == 0:
                    pe.wait_ge(stack_loaded[i], 96 * r + 96)
                if half == 0 and not (isinstance(n, int) and n < 2):
                    pe.wait_ge(max_done, n - 1)
                at = (2 * (u % 2) + half) * P
                mm = pe.matmul(sa_ps[:, u % 2, half, :], q_stack[i][0:PAD, u // 2, at:at + P],
                               k_stack[i][0:PAD, u // 2, :], start=True, stop=True)
                if half == 1:
                    mm.then_inc(sa_done, 1)

            def scores_t(s, c, j):
                n = 16 * s.g + HG * c + j
                if c == 0 and j == 0:
                    pe.wait_ge(max_rows[s.q], 32 * s.r + 32)
                if not (isinstance(n, int) and n < 2):
                    pe.wait_ge(exp_done, n - 1)
                pe.matmul(sb_ps[:, j % 2, :], k_stack[s.q][0:PAD + 2, j, c * P:(c + 1) * P],
                          q_stack[s.q][0:PAD + 2, j, :], start=True, stop=True).then_inc(sb_done, 1)

            def by_values(q, g, c):
                if c == 0:
                    pe.wait_ge(vt_done, g + 1)
                    if not (isinstance(g, int) and g == 0):
                        pe.wait_ge(o_done, g)
                pe.wait_ge(exp_done, 16 * g + 4 * c + 4)
                for j in range(HG):
                    mm = pe.matmul(o_ps[32 * j:32 * j + 32, :], v_t[q % 2][:, c, j, :], probs[:, c % 2, j, :],
                                   start=(c == 0), stop=(c == KC - 1))
                mm.then_inc(pv_done, 1)

            def values_and_maxima(q, g, b):
                pe.wait_ge(v_loaded[q % 2], 16 * b + 16)
                pe.wait_ge(max_done, 8 * g + 8)
                pe.transpose(m_ps[0:4 * HG, 256:384], maxima[q % 2][:, :], ident[:, :])
                for c in range(KC):
                    mm = pe.transpose(m_ps[:, c * GR:(c + 1) * GR], v_rows[q % 2][:, c * P:(c + 1) * P], ident[0:GR, 0:GR])
                mm.then_inc(vm_done, 1)

            def outputs_t(g):
                pe.wait_ge(o_done, g + 1)
                for c in range(KC):
                    mm = pe.transpose(m_ps[:, c * P:(c + 1) * P], o_sb[:, c * P:(c + 1) * P], ident[:, :])
                mm.then_inc(ot_done, 1)

            def back(b):
                pe.wait_ge(norm_done, 2 * b + 2)
                for c in range(KC):
                    mm = pe.transpose(m_ps[:, c * P:(c + 1) * P], attn_t[:, c, :], ident[:, :])
                mm.then_inc(back_done, 1)

            def normed_t(b):
                pe.wait_ge(yn_done, b + 1)
                for c in range(KC):
                    mm = pe.transpose(m_ps[:, c * P:(c + 1) * P], yn[:, c * P:(c + 1) * P], ident[:, :])
                mm.then_inc(ynt_done, 1)

            ORDER = (("TSTSTSTSV", "TSTSOTSTSV", "TSTSMTSTSV", "TSTSBTSTSV"),
                     ("TSTSSSTTV", "TSTSOTSTSVN", "TSTSMTSTSV", "TSTSSSTTV"))

            def slot(s):
                q, g, r = s.q, s.g, s.r
                q1, q2 = (q + 1) % 4, (q + 2) % 4
                for c in range(KC):
                    j = n = 0
                    for step in ORDER[q % 2][c]:
                        if step == "T":
                            scores_t(s, c, j)
                            j += 1
                        elif step == "S":
                            u, half = 2 * c + n // 2 + (4 if c < 2 else -4), n % 2
                            n += 1
                            if c < 2 and s.before(NG - 1):
                                scores(q1, g + 1, r + (q + 1) // 4, u, half)
                            if c >= 2 and s.before(NG - 2):
                                scores(q2, g + 2, r + (q + 2) // 4, u, half)
                        elif step == "V" and c > 0:
                            by_values(q, g, c - 1)
                        elif step == "V" and s.at_least(1):
                            by_values((q - 1) % 4, g - 1, KC - 1)
                        elif step == "O" and s.at_least(1):
                            if q % 2 == 1 and s.at_least(3):
                                pe.wait_ge(y_done, 2 * r + q // 2)
                            else:
                                pe.wait_ge(vt_done, g + 1)
                            outputs_t(g - 1)
                        elif step == "N" and has_late(s):
                            pe.wait_ge(norm_done, g)
                            normed_t(batch_late(s))
                        elif step == "M" and s.before(NG - 1):
                            if has_late(s):
                                pe.wait_ge(yn32_done, batch_late(s) + 1)
                            elif s.at_least(1):
                                pe.wait_ge(norm_done, g)
                            else:
                                pe.wait_ge(vt_done, 1)
                            values_and_maxima(q1, g + 1, 2 * r + (q + 1) // 2)
                        elif step == "B" and has_back(s):
                            pe.wait_ge(vt_done, g + 2)
                            back(batch_back(s))

            for u in range(8):
                for half in range(2):
                    scores(0, 0, 0, u, half)
            for u in range(2):
                for half in range(2):
                    scores(1, 1, 0, u, half)
            values_and_maxima(0, 0, 0)
            for u in range(2, 4):
                for half in range(2):
                    scores(1, 1, 0, u, half)
            slots(pe, slot)
            by_values(3, NG - 1, KC - 1)
            pe.wait_ge(ex.w_lo_done, 1)
            pe.wait_ge(ynlo_done, 8)
            pe.wait_ge(max_done, 8 * NG)
            ex.first_products(pe, first_chunk, 0, 0, 0)
            pe.wait_ge(yn32_done, B - 1)
            outputs_t(NG - 1)
            pe.wait_ge(ex.w_lo_done, 2)
            ex.first_products(pe, first_chunk, 0, 0, 1)
            pe.wait_ge(norm_done, NG)
            back(B - 1)
            for piece in range(2):
                ex.first_products(pe, first_chunk, 1, 0, piece)
            pe.wait_ge(y_done, B)
            normed_t(B - 1)

        attn.close()
        experts(nc, whole, sem, ex, y_all, ident, w_r, tanh_g, out)


def experts(nc, whole, sem, ex, y_all, ident, w_r, tanh_g, out):
    B, TOK, D = out.shape
    NE, FE, KC, SPAN, NT, HALF = ex.NE, ex.FE, ex.KC, ex.SPAN, ex.NT, ex.HALF
    TT = SPAN // TOK
    TOP = 4
    NCOL = NE + 1
    NSH = ex.FS // FE
    NCH = 1 + NSH + NE
    assert HALF == P and NSH == 5 and FE == 2 * P and NT == 4 and TT == 4

    stack = whole.enter_context(ExitStack())
    sb = lambda name, shape, dt=F32: stack.enter_context(nc.sbuf_tensor(name, shape, dt))
    ps = lambda name, shape, dt=F32: stack.enter_context(nc.psum_tensor(name, shape, dt))

    ex.w_raw.append(sb("w_raw1", [P, 3, KC * FE]))
    ex.w_split.append(sb("w_split1", [P, 2, 3, KC * FE], F32R))
    w_raw, w_split, g_ps, u_ps = ex.w_raw, ex.w_split, ex.g_ps, ex.u_ps
    h_split = [sb(f"h_split{i}", [P, 2, 2, SPAN], F32R) for i in range(2)]
    th = [sb(f"th{i}", [P, SPAN]) for i in range(2)]
    gated = [sb(f"gated{i}", [P, SPAN]) for i in range(2)]
    hid = [sb(f"hid{i}", [P, SPAN]) for i in range(2)]
    col = [sb(f"col{i}", [P, B]) for i in range(2)]
    logits_t = sb("logits_t", [P, SPAN])
    logits = sb("logits", [P, B, NCOL])
    top_v = sb("top_v", [P, B, 8])
    top_i = sb("top_i", [P, B, 8], U32)
    top_f = sb("top_f", [P, B, TOP])
    less = sb("less", [P, B, TOP])
    e_top = sb("e_top", [P, B, TOP])
    e_sum = sb("e_sum", [P, B, 1])
    e_rec = sb("e_rec", [P, B, 1])
    w_top = sb("w_top", [P, B, TOP])
    ids = sb("ids", [P, NE, B])
    hit = sb("hit", [P, NE, B])
    term = sb("term", [P, NE, B])
    scale = sb("scale", [P, NCOL, B])
    th_gate = sb("th_gate", [P, B])

    d_ps = [ps(f"d_ps{i}", [P, D]) for i in range(4)]

    w_loaded, w_hi_done, w_lo_done, g_done, u_done = ex.w_loaded, ex.w_hi_done, ex.w_lo_done, ex.g_done, ex.u_done
    s_ids, s_route, s_routed, s_etop, s_thg = sem("s_ids"), sem("s_route"), sem("s_routed"), sem("s_etop"), sem("s_thg")
    th_done, gated_done, hid_done, h_hi_done, h_lo_done = (sem(n) for n in ("th_done", "gated_done", "hid_done", "h_hi_done", "h_lo_done"))
    d_done, acc_done = sem("d_done"), sem("acc_done")
    col_done = sem("col_done")
    router_done, logits_t_done, turned, logits_done = sem("router_done"), sem("logits_t_done"), sem("turned"), sem("logits_done")
    out_stored = sem("out_stored")

    def chunks(eng, one):
        one(Chunk(0, 0, ex), "shared", 0)
        one(Chunk(1, 1, ex), "shared", HALF)
        with eng.Fori(0, (NSH - 1) // 2) as i:
            for j in range(2):
                one(Chunk(2 * i + 2 + j, j, ex), "shared", (2 * i + 1 + j) * FE + HALF)
        with eng.Fori(0, NE // 2) as i:
            for j in range(2):
                one(Chunk(2 * i + 1 + NSH + j, j, ex), "expert", 2 * i + j)

    def chunks_ahead(eng, one):
        one(Chunk(0, 0, ex), (Chunk(1, 1, ex), 0))
        one(Chunk(1, 1, ex), (Chunk(2, 0, ex), 1))
        with eng.Fori(0, (NCH - 4) // 2) as i:
            for j in range(2):
                one(Chunk(2 * i + 2 + j, j, ex), (Chunk(2 * i + 3 + j, 1 - j, ex), i + 1 + j))
        one(Chunk(NCH - 2, 0, ex), (Chunk(NCH - 1, 1, ex), (NCH - 1) // 2))
        one(Chunk(NCH - 1, 1, ex), None)

    block = whole.enter_context(nc.Block())

    @block.sync
    def _(sp):
        def load(c, kind, at):
            if not (isinstance(c.n, int) and c.n == 0):
                ex.load_weights(sp, c, kind, at)

        chunks(sp, load)
        rows = out.rearrange("b p d -> p b d")
        for t in range(NT - 1):
            sp.wait_ge(acc_done, 4 * (4 * (NCH - 1) + t) + 4)
            sp.dma_start(rows[:, t * TT:(t + 1) * TT, :],
                         y_all[:, t * TT * D:(t + 1) * TT * D].rearrange("p (b d) -> p b d", b=TT)).then_inc(out_stored, 16)
        for b in range(B - TT, B):
            sp.wait_ge(acc_done, 16 * (NCH - 1) + b + 1)
            sp.dma_start(out[b], y_all[:, b * D:(b + 1) * D]).then_inc(out_stored, 16)
        sp.wait_ge(out_stored, 16 * (NT - 1 + TT))

    @block.gpsimd
    def _(pool):
        pool.iota(ids[:, :, :], pattern=[[1, NE], [0, B]], base=0, channel_multiplier=0,
                  allow_small_or_imprecise_dtypes=True).then_inc(s_ids, 1)

        def hidden(c, following):
            for t in range(NT):
                for f in range(c.tiles):
                    pool.wait_ge(h_hi_done, c.tile(t, f) + 1)
                    pool.tensor_tensor(h_split[t % 2][:, 1, f, :], hid[c.slot(t, f)][:, :],
                                       h_split[t % 2][:, 0, f, :].bitcast(F32), ALU.subtract).then_inc(h_lo_done, 1)
                if t < 3 and following:
                    ex.lower_weights(pool, following[0], t)

        chunks_ahead(pool, hidden)

    @block.scalar
    def _(act):
        def upper_half(c, half, i):
            if i == 0:
                act.wait_ge(w_loaded[c.j], 48 * half + 48)
                if not (isinstance(c.n, int) and c.n < 2):
                    act.wait_ge(d_done, 16 * c.n - 16)
            ex.upper_weights(act, c, i)

        def hidden(c, following):
            for t in range(NT):
                for f in range(c.tiles):
                    y, i = c.tile(t, f), c.slot(t, f)
                    act.wait_ge(g_done, y + 1)
                    if not (isinstance(y, int) and y < 2):
                        act.wait_ge(gated_done, y - 1)
                    act.activation(th[i][:, :], g_ps[i], ACT.Tanh, scale=0.5).then_inc(th_done, 1)
                    act.wait_ge(hid_done, y + 1)
                    x = c.unit(t)
                    if not (isinstance(x, int) and x < 2):
                        act.wait_ge(d_done, 4 * x - 4)
                    act.activation(h_split[t % 2][:, 0, f, :], hid[i][:, :], ACT.Copy).then_inc(h_hi_done, 1)
                if t < 3 and following:
                    upper_half(*following, t)
                if isinstance(c.n, int) and c.n == 0 and t == 0:
                    act.wait_ge(router_done, 1)
                    act.activation(logits_t[:, :], d_ps[3][:, :], ACT.Copy).then_inc(logits_t_done, 1)
                if isinstance(c.n, int) and c.n == 0 and t == 1:
                    act.wait_ge(logits_done, 1)
                    act.activation(th_gate[:, :], logits[:, :, NE], ACT.Tanh, scale=0.5).then_inc(s_thg, 1)
                if isinstance(c.n, int) and c.n == 0 and t == 3:
                    act.wait_ge(s_route, 1)
                    act.activation(e_top[:, :, :], less[:, :, :], ACT.Exp).then_inc(s_etop, 1)

        chunks_ahead(act, hidden)

    @block.vector
    def _(dve):
        n_steps = [0]

        def step(ins):
            ins.then_inc(s_routed, 1)
            n_steps[0] += 1
            dve.wait_ge(s_routed, n_steps[0])

        def keep_logits():
            dve.wait_ge(turned, 1)
            dve.tensor_copy(logits[:, :, :].rearrange("p (t i) e -> p i t e", t=NT),
                            g_ps[0].rearrange("p (i t e) -> p i t e", i=TT, t=NT)[:, :, :, 0:NCOL]).then_inc(logits_done, 1)

        def gate():
            dve.wait_ge(s_thg, 1)
            step(dve.tensor_scalar(th_gate[:, :], th_gate[:, :], 0.5, 0.5, ALU.mult, ALU.add))
            step(dve.tensor_scalar(scale[:, NE, :], th_gate[:, :], tanh_g[:, 1:2], None, ALU.mult))

        def largest():
            for b in range(B):
                dve.max(top_v[:, b, :], logits[:, b, 0:NE]).then_inc(s_routed, 1)
            n_steps[0] += B
            dve.wait_ge(s_routed, n_steps[0])
            dve.tensor_tensor(less[:, :, :], top_v[:, :, 0:TOP], top_v[:, :, 0:1].to_broadcast([P, B, TOP]),
                              ALU.subtract).then_inc(s_route, 1)

        def places():
            for b in range(B):
                dve.max_index(top_i[:, b, :], top_v[:, b, :], logits[:, b, 0:NE]).then_inc(s_routed, 1)
            n_steps[0] += B
            dve.wait_ge(s_routed, n_steps[0])
            step(dve.tensor_copy(top_f[:, :, :], top_i[:, :, 0:TOP]))

        def weights():
            dve.wait_ge(s_etop, 1)
            step(dve.tensor_reduce(e_sum[:, :, :].rearrange("p b o -> p (b o)"), e_top[:, :, :], AX_X, ALU.add))
            step(dve.reciprocal(e_rec[:, :, :], e_sum[:, :, :]))
            step(dve.tensor_scalar(e_rec[:, :, :], e_rec[:, :, :], tanh_g[:, 1:2], None, ALU.mult))
            step(dve.tensor_tensor(w_top[:, :, :], e_top[:, :, :], e_rec[:, :, :].to_broadcast([P, B, TOP]), ALU.mult))
            dve.wait_ge(s_ids, 1)

        def spread(ks):
            for k in ks:
                across = lambda t: t[:, :, k:k + 1].rearrange("p b o -> p o b").to_broadcast([P, NE, B])
                step(dve.tensor_tensor(hit[:, :, :], ids[:, :, :], across(top_f), ALU.is_equal))
                if k == 0:
                    step(dve.tensor_tensor(scale[:, 0:NE, :], hit[:, :, :], across(w_top), ALU.mult))
                else:
                    step(dve.tensor_tensor(term[:, :, :], hit[:, :, :], across(w_top), ALU.mult))
                    step(dve.tensor_tensor(scale[:, 0:NE, :], scale[:, 0:NE, :], term[:, :, :], ALU.add))

        def routing(n, t):
            part = 4 * n + t
            if part == 1:
                largest()
            elif part == 3:
                places()
            elif part == 4:
                weights()
            elif part in (5, 6):
                spread((2 * part - 10, 2 * part - 9))

        def accumulate(c, t):
            x = c.unit(t)
            for i in range(TT):
                dve.wait_ge(d_done, 4 * x + i + 1)
                if i == 0 and t == 0:
                    dve.wait_ge(col_done, c.n + 1)
                if not (isinstance(x, int) and x < 4):
                    dve.wait_ge(acc_done, 4 * x + i - 15)
                y_b = y_all[:, (t * TT + i) * D:(t * TT + i + 1) * D]
                dve.scalar_tensor_tensor(out=y_b, in0=d_ps[i][:, :], scalar=col[c.j][:, t * TT + i:t * TT + i + 1],
                                         in1=y_b, op0=ALU.mult, op1=ALU.add).then_inc(acc_done, 1)

        def hidden(c, kind, at):
            src = scale[:, NE, :] if kind == "shared" else scale[:, bass.ds(at, 1), :].rearrange("p o b -> p (o b)")
            for t in range(NT):
                for f in range(c.tiles):
                    y, i = c.tile(t, f), c.slot(t, f)
                    dve.wait_ge(th_done, y + 1)
                    dve.scalar_tensor_tensor(out=gated[i][:, :], in0=th[i][:, :], scalar=1.0, in1=g_ps[i],
                                             op0=ALU.add, op1=ALU.mult).then_inc(gated_done, 1)
                    dve.wait_ge(gated_done, y + 1)
                    dve.wait_ge(u_done, y + 1)
                    if not (isinstance(y, int) and y < 2):
                        dve.wait_ge(h_lo_done, y - 1)
                    dve.scalar_tensor_tensor(out=hid[i][:, :], in0=gated[i][:, :], scalar=0.5, in1=u_ps[i],
                                             op0=ALU.mult, op1=ALU.mult).then_inc(hid_done, 1)
                first = isinstance(c.n, int) and c.n == 0
                if first and t == 1:
                    keep_logits()
                    gate()
                    dve.tensor_copy(col[c.j][:, :], src).then_inc(col_done, 1)
                if c.before(t):
                    accumulate(*c.before(t))
                if t == 0 and not first:
                    dve.tensor_copy(col[c.j][:, :], src).then_inc(col_done, 1)
                if isinstance(c.n, int):
                    routing(c.n, t)

        chunks(dve, hidden)
        accumulate(Chunk(NCH - 1, 1, ex), NT - 1)

    @block.tensor
    def _(pe):
        def first_products(c, t, f):
            y = c.tile(t, f)
            if t == 0 and f == 0:
                pe.wait_ge(w_lo_done, 3 * c.n + 2)
            if not (isinstance(y, int) and y < 2):
                pe.wait_ge(hid_done, y - 1)
            if isinstance(y, int) and y == 2:
                pe.wait_ge(logits_done, 1)
            for piece in range(2):
                ex.first_products(pe, c, t, f, piece)

        def router():
            for n, (a, k) in enumerate((a, k) for a in range(2) for k in range(KC)):
                for t in range(NT):
                    mm = pe.matmul(d_ps[3][32 * t:32 * t + 32, :], w_r[:, k, :],
                                   ex.yn_t[:, a, k, t * SPAN:(t + 1) * SPAN].bitcast(F32), start=(n == 0), stop=(n == 2 * KC - 1))
            mm.then_inc(router_done, 1)

        def turn_logits():
            pe.wait_ge(logits_t_done, 1)
            pe.wait_ge(gated_done, 1)
            pe.wait_ge(hid_done, 1)
            for i in range(TT):
                mm = pe.transpose(g_ps[0][:, i * P:(i + 1) * P], logits_t[:, i * P:(i + 1) * P], ident[:, :])
            mm.then_inc(turned, 1)

        def down(c, t):
            x = c.unit(t)
            if t == 0:
                pe.wait_ge(w_lo_done, 3 * c.n + 3)
            pe.wait_ge(h_lo_done, c.tile(t, c.tiles - 1) + 1)
            for i in range(TT):
                if isinstance(x, int) and x == 0 and i == 2:
                    turn_logits()
                if not (isinstance(x, int) and x < 1):
                    pe.wait_ge(acc_done, 4 * x + i - 3)
                n = 0
                for f in range(c.tiles):
                    for a, b in ex.TERMS:
                        w = c.piece(w_split[c.j][:, b], 2).rearrange("p (k d) -> p k d", d=D)
                        mm = pe.matmul(d_ps[i][:, :], h_split[t % 2][:, a, f, i * P:(i + 1) * P], w[:, f, :],
                                       start=(n == 0), stop=(n == 3 * c.tiles - 1))
                        n += 1
                mm.then_inc(d_done, 1)

        def chunk(c, kind, at):
            for t in range(NT):
                for f in range(c.tiles):
                    if not (isinstance(c.n, int) and c.n == 0 and t < 2):
                        first_products(c, t, f)
                if c.before(t):
                    down(*c.before(t))

        router()
        chunks(pe, chunk)
        down(Chunk(NCH - 1, 1, ex), NT - 1)


_INS = ['x', 'ctx_2048', 'g_xattn', 'g_ffn', 'L0_ffn_w_router', 'L0_ffn_w_gate', 'L0_ffn_w_up', 'L0_ffn_w_down',
        'L0_ffn_w_sh_gate', 'L0_ffn_w_sh_up', 'L0_ffn_w_sh_down', 'L0_ffn_w_sh_expert_gate']


def kernel(**inputs):
    import numpy as _np
    import concourse.bacc as _bacc
    from concourse import mybir as _mybir
    from concourse.bass_utils import run_bass_kernel_spmd as _run

    nc = _bacc.Bacc("TRN2", target_bir_lowering=False, num_devices=1)
    arrays, args = {}, []
    for name in _INS:
        a = _np.ascontiguousarray(inputs[name])
        arrays[f"in_{name}_dram"] = a
        args.append(nc.dram_tensor(f"in_{name}_dram", a.shape, _mybir.dt.from_np(a.dtype), kind="ExternalInput").ap())
    shape = tuple(inputs['x'].shape)
    args.append(nc.dram_tensor("out_0_dram", shape, _mybir.dt.float32, kind="ExternalOutput").ap())
    gated_block(nc, *args)
    r = _run(nc, [arrays], core_ids=[0])
    return r.results[0]["out_0_dram"]
```
